# Optimizing a Trainium2 kernel written in Bass

```python
import numpy as np
import jax
import jax.numpy as jnp

def _softmax(x, axis=-1):
    return jax.nn.softmax(x, axis=axis)

def _gelu(x):
    return jax.nn.gelu(x, approximate=True)

def _silu(x):
    return jax.nn.silu(x)

def _sigmoid(x):
    return jax.nn.sigmoid(x)

def _layernorm(x, axis=-1, eps=1e-05):
    m = jnp.mean(x, axis=axis, keepdims=True)
    v = jnp.var(x, axis=axis, keepdims=True)
    return (x - m) / jnp.sqrt(v + eps)

def _scatter_add(tgt, idx, src, axis=0):
    return tgt.at[idx].add(src)

def _segment_sum(src, seg, n):
    return jax.ops.segment_sum(src, seg, n)
kernel_name = 'mk_hybrid_d2_jaxref_r8_92e97d'

def setup_inputs(seed: int=0):
    np.random.seed(seed)
    _w = jnp.asarray

    def _L0_attn_a_setup():
        import jax, jax.numpy as jnp
        import numpy as np
        B, L, D = (2, 256, 128)
        H, HD = (16, 64)
        LD = 32
        key = jax.random.key(seed)
        ks = jax.random.split(key, 6)
        s = lambda fan_in: 1.0 / np.sqrt(fan_in)
        x_bld = jax.random.normal(ks[0], (B, L, D), dtype=jnp.float32)
        Wq = jax.random.normal(ks[1], (D, H, HD), dtype=jnp.float32) * s(D)
        Wkv_down = jax.random.normal(ks[2], (D, LD), dtype=jnp.float32) * s(D)
        Wk_up = jax.random.normal(ks[3], (LD, H, HD), dtype=jnp.float32) * s(LD)
        Wv_up = jax.random.normal(ks[4], (LD, H, HD), dtype=jnp.float32) * s(LD)
        Wout = jax.random.normal(ks[5], (H, HD, D), dtype=jnp.float32) * s(H * HD)
        return {'x_bld': x_bld, 'Wq': Wq, 'Wkv_down': Wkv_down, 'Wk_up': Wk_up, 'Wv_up': Wv_up, 'Wout': Wout}
    _L0_attn_a_in = _L0_attn_a_setup()

    def _L0_attn_b_setup():
        import jax, jax.numpy as jnp
        import numpy as np
        B_, L_, D_, E_, N_, DT_, K_ = (2, 128, 128, 256, 16, 64, 4)
        EPS = 1e-05

        def _forward(resid, norm_w, skip_w, in_w, conv_w, conv_b, wd1, wd2, wd2_b, wb, wc, A_log, W_D, out_w):
            B, L, D = resid.shape
            E, N = A_log.shape
            K = conv_w.shape[-1]
            xn = resid * jax.lax.rsqrt(jnp.mean(resid * resid, -1, keepdims=True) + EPS) * norm_w
            skip = jnp.einsum('bld,ed->ble', xn, skip_w)
            x = jnp.einsum('bld,ed->ble', xn, in_w)
            xp = jnp.pad(x, ((0, 0), (K - 1, 0), (0, 0)))
            conv = conv_b + sum((xp[:, k:k + L, :] * conv_w[:, k] for k in range(K)))
            x = jax.nn.silu(conv)
            delta = jax.nn.softplus(jnp.einsum('ble,re->blr', x, wd1) @ wd2.T + wd2_b)
            Bt = jnp.einsum('ble,ne->bln', x, wb)
            Ct = jnp.einsum('ble,ne->bln', x, wc)
            A = -jnp.exp(A_log)

            def step(h, inp):
                dt, b_t, c_t, x_t = inp
                A_bar = jnp.exp(dt[:, :, None] * A)
                h = A_bar * h + (dt * x_t)[:, :, None] * b_t[:, None, :]
                y = jnp.einsum('ben,bn->be', h, c_t)
                return (h, y)
            h0 = jnp.zeros((B, E, N), x.dtype)
            xs = (delta.transpose(1, 0, 2), Bt.transpose(1, 0, 2), Ct.transpose(1, 0, 2), x.transpose(1, 0, 2))
            _, y = jax.lax.scan(step, h0, xs)
            y = y.transpose(1, 0, 2)
            y = y + x * W_D
            y = y * jax.nn.silu(skip)
            y = jnp.einsum('ble,de->bld', y, out_w)
            return resid + y
        key = jax.random.key(seed)
        ks = jax.random.split(key, 16)
        s = lambda *sh: 1.0 / np.sqrt(sh[-1])
        return {'resid': jax.random.normal(ks[0], (B_, L_, D_), jnp.float32), 'norm_w': jnp.ones((D_,), jnp.float32), 'skip_w': jax.random.normal(ks[1], (E_, D_), jnp.float32) * s(E_, D_), 'in_w': jax.random.normal(ks[2], (E_, D_), jnp.float32) * s(E_, D_), 'conv_w': jax.random.normal(ks[3], (E_, K_), jnp.float32) * s(E_, K_), 'conv_b': jax.random.normal(ks[4], (E_,), jnp.float32) * 0.1, 'wd1': jax.random.normal(ks[5], (DT_, E_), jnp.float32) * s(DT_, E_), 'wd2': jax.random.normal(ks[6], (E_, DT_), jnp.float32) * s(E_, DT_), 'wd2_b': jax.random.normal(ks[7], (E_,), jnp.float32) * 0.1, 'wb': jax.random.normal(ks[8], (N_, E_), jnp.float32) * s(N_, E_), 'wc': jax.random.normal(ks[9], (N_, E_), jnp.float32) * s(N_, E_), 'A_log': jnp.log(jax.random.uniform(ks[10], (E_, N_), jnp.float32, 0.5, 4.0)), 'W_D': jnp.ones((E_,), jnp.float32), 'out_w': jax.random.normal(ks[11], (D_, E_), jnp.float32) * s(D_, E_)}
    _L0_attn_b_in = _L0_attn_b_setup()

    def _L0_ffn_setup():
        import jax, jax.numpy as jnp
        import numpy as np
        import math
        BETA = 0.9
        THRESHOLD = 1.0
        NUM_STEPS = 5
        ALPHA = 2.0

        @jax.custom_vjp
        def spike_fn(u):
            return (u > 0).astype(u.dtype)

        def _spike_fwd(u):
            return (spike_fn(u), u)

        def _spike_bwd(u, g):
            s = jnp.pi / 2.0 * ALPHA * u
            return (g * (ALPHA / 2.0) / (1.0 + s * s),)
        spike_fn.defvjp(_spike_fwd, _spike_bwd)
        key = jax.random.key(seed)
        k1, k2, k3 = jax.random.split(key, 3)
        n_embd = 128
        x = jax.random.normal(k1, (4, 256, n_embd), dtype=jnp.float32)
        W_fc = jax.random.normal(k2, (4 * n_embd, n_embd), dtype=jnp.float32) / math.sqrt(n_embd)
        W_proj = jax.random.normal(k3, (n_embd, 4 * n_embd), dtype=jnp.float32) / math.sqrt(4 * n_embd)
        return {'x': x, 'W_fc': W_fc, 'W_proj': W_proj}
    _L0_ffn_in = _L0_ffn_setup()

    def _L1_attn_a_setup():
        import jax, jax.numpy as jnp
        import numpy as np
        HEADS = 4
        DIM_HEAD = 32
        EPS = 1e-05
        key = jax.random.key(seed)
        ks = jax.random.split(key, 6)
        b, n, dim = (8, 512, 128)
        hidden = HEADS * DIM_HEAD
        x = jax.random.normal(ks[0], (b, n, dim), dtype=jnp.float32)
        gamma = jnp.ones((1, 1, dim), dtype=jnp.float32)
        beta = jnp.zeros((1, 1, dim), dtype=jnp.float32)
        w_qkv = jax.random.normal(ks[1], (dim, hidden * 3), dtype=jnp.float32) / np.sqrt(dim)
        w_out = jax.random.normal(ks[2], (hidden, dim), dtype=jnp.float32) / np.sqrt(hidden)
        b_out = jnp.zeros((dim,), dtype=jnp.float32)
        return {'x': x, 'gamma': gamma, 'beta': beta, 'w_qkv': w_qkv, 'w_out': w_out, 'b_out': b_out}
    _L1_attn_a_in = _L1_attn_a_setup()

    def _L1_attn_b_setup():
        import jax, jax.numpy as jnp
        import numpy as np
        HIDDEN = 128
        N_HEADS = 16
        HEAD_DIM = HIDDEN // N_HEADS
        SCALE = HEAD_DIM ** (-0.5)
        key = jax.random.key(seed)
        k1, k2, k3 = jax.random.split(key, 3)
        x = jax.random.normal(k1, (2, 256, HIDDEN), dtype=jnp.float32)
        w_qkv = jax.random.normal(k2, (HIDDEN, 3 * HIDDEN), dtype=jnp.float32) * HIDDEN ** (-0.5)
        b_qkv = jnp.zeros((3 * HIDDEN,), dtype=jnp.float32)
        w_proj = jax.random.normal(k3, (HIDDEN, HIDDEN), dtype=jnp.float32) * HIDDEN ** (-0.5)
        b_proj = jnp.zeros((HIDDEN,), dtype=jnp.float32)
        return {'x': x, 'w_qkv': w_qkv, 'b_qkv': b_qkv, 'w_proj': w_proj, 'b_proj': b_proj}
    _L1_attn_b_in = _L1_attn_b_setup()

    def _L1_ffn_setup():
        import jax, jax.numpy as jnp
        import numpy as np
        NUM_EXPERTS = 8
        HIDDEN = 128
        FFN = 512
        BATCH = 2
        SEQ = 256
        key = jax.random.key(seed)
        k_x, k_g, k_u, k_d = jax.random.split(key, 4)
        scale_in = 1.0 / np.sqrt(HIDDEN)
        scale_mid = 1.0 / np.sqrt(FFN)
        return {'hidden_states': jax.random.normal(k_x, (BATCH, SEQ, HIDDEN), dtype=jnp.float32), 'Wg': jax.random.normal(k_g, (NUM_EXPERTS, HIDDEN, FFN), dtype=jnp.float32) * scale_in, 'Wu': jax.random.normal(k_u, (NUM_EXPERTS, HIDDEN, FFN), dtype=jnp.float32) * scale_in, 'Wd': jax.random.normal(k_d, (NUM_EXPERTS, FFN, HIDDEN), dtype=jnp.float32) * scale_mid}
    _L1_ffn_in = _L1_ffn_setup()
    _d = {'L0_attn_a_x_bld': _L0_attn_a_in['x_bld'], 'L0_attn_a_Wq': _L0_attn_a_in['Wq'], 'L0_attn_a_Wkv_down': _L0_attn_a_in['Wkv_down'], 'L0_attn_a_Wk_up': _L0_attn_a_in['Wk_up'], 'L0_attn_a_Wv_up': _L0_attn_a_in['Wv_up'], 'L0_attn_a_Wout': _L0_attn_a_in['Wout'], 'L0_attn_b_norm_w': _L0_attn_b_in['norm_w'], 'L0_attn_b_skip_w': _L0_attn_b_in['skip_w'], 'L0_attn_b_in_w': _L0_attn_b_in['in_w'], 'L0_attn_b_conv_w': _L0_attn_b_in['conv_w'], 'L0_attn_b_conv_b': _L0_attn_b_in['conv_b'], 'L0_attn_b_wd1': _L0_attn_b_in['wd1'], 'L0_attn_b_wd2': _L0_attn_b_in['wd2'], 'L0_attn_b_wd2_b': _L0_attn_b_in['wd2_b'], 'L0_attn_b_wb': _L0_attn_b_in['wb'], 'L0_attn_b_wc': _L0_attn_b_in['wc'], 'L0_attn_b_A_log': _L0_attn_b_in['A_log'], 'L0_attn_b_W_D': _L0_attn_b_in['W_D'], 'L0_attn_b_out_w': _L0_attn_b_in['out_w'], 'L0_ffn_W_fc': _L0_ffn_in['W_fc'], 'L0_ffn_W_proj': _L0_ffn_in['W_proj'], 'L1_attn_a_gamma': _L1_attn_a_in['gamma'], 'L1_attn_a_beta': _L1_attn_a_in['beta'], 'L1_attn_a_w_qkv': _L1_attn_a_in['w_qkv'], 'L1_attn_a_w_out': _L1_attn_a_in['w_out'], 'L1_attn_a_b_out': _L1_attn_a_in['b_out'], 'L1_attn_b_w_qkv': _L1_attn_b_in['w_qkv'], 'L1_attn_b_b_qkv': _L1_attn_b_in['b_qkv'], 'L1_attn_b_w_proj': _L1_attn_b_in['w_proj'], 'L1_attn_b_b_proj': _L1_attn_b_in['b_proj'], 'L1_ffn_Wg': _L1_ffn_in['Wg'], 'L1_ffn_Wu': _L1_ffn_in['Wu'], 'L1_ffn_Wd': _L1_ffn_in['Wd']}
    _x0 = _d['L0_attn_a_x_bld']
    _d['L0_attn_a_x_bld'] = jax.random.normal(jax.random.fold_in(jax.random.key(seed), 1), (2, 1024, 128), dtype=_x0.dtype)
    del _x0
    return _d

def reference(L0_attn_a_x_bld, L0_attn_a_Wq, L0_attn_a_Wkv_down, L0_attn_a_Wk_up, L0_attn_a_Wv_up, L0_attn_a_Wout, L0_attn_b_norm_w, L0_attn_b_skip_w, L0_attn_b_in_w, L0_attn_b_conv_w, L0_attn_b_conv_b, L0_attn_b_wd1, L0_attn_b_wd2, L0_attn_b_wd2_b, L0_attn_b_wb, L0_attn_b_wc, L0_attn_b_A_log, L0_attn_b_W_D, L0_attn_b_out_w, L0_ffn_W_fc, L0_ffn_W_proj, L1_attn_a_gamma, L1_attn_a_beta, L1_attn_a_w_qkv, L1_attn_a_w_out, L1_attn_a_b_out, L1_attn_b_w_qkv, L1_attn_b_b_qkv, L1_attn_b_w_proj, L1_attn_b_b_proj, L1_ffn_Wg, L1_ffn_Wu, L1_ffn_Wd):

    def _L0_attn_a_ref(x_bld, Wq, Wkv_down, Wk_up, Wv_up, Wout):
        import jax, jax.numpy as jnp
        import numpy as np
        B, L, D = (2, 256, 128)
        H, HD = (16, 64)
        LD = 32
        q_blhd = jnp.einsum('bld,dhk->blhk', x_bld, Wq)
        latent_bll = jnp.einsum('bld,dc->blc', x_bld, Wkv_down)
        k_blhd = jnp.einsum('blc,chk->blhk', latent_bll, Wk_up)
        v_blhd = jnp.einsum('blc,chk->blhk', latent_bll, Wv_up)
        attn = jnp.einsum('bqhd,bkhd->bhqk', q_blhd, k_blhd) / jnp.sqrt(jnp.asarray(HD, dtype=x_bld.dtype))
        l = x_bld.shape[1]
        mask = (jnp.arange(l)[None, :] <= jnp.arange(l)[:, None])[None, None]
        neg_inf = jnp.finfo(attn.dtype).min
        attn = jax.nn.softmax(jnp.where(mask, attn, neg_inf), axis=-1)
        y_blhd = jnp.einsum('bhqk,bkhd->bqhd', attn, v_blhd)
        return jnp.einsum('bqhd,hdo->bqo', y_blhd, Wout)

    def _L0_attn_b_ref(resid, norm_w, skip_w, in_w, conv_w, conv_b, wd1, wd2, wd2_b, wb, wc, A_log, W_D, out_w):
        import jax, jax.numpy as jnp
        import numpy as np
        B_, L_, D_, E_, N_, DT_, K_ = (2, 128, 128, 256, 16, 64, 4)
        EPS = 1e-05

        def _forward(resid, norm_w, skip_w, in_w, conv_w, conv_b, wd1, wd2, wd2_b, wb, wc, A_log, W_D, out_w):
            B, L, D = resid.shape
            E, N = A_log.shape
            K = conv_w.shape[-1]
            xn = resid * jax.lax.rsqrt(jnp.mean(resid * resid, -1, keepdims=True) + EPS) * norm_w
            skip = jnp.einsum('bld,ed->ble', xn, skip_w)
            x = jnp.einsum('bld,ed->ble', xn, in_w)
            xp = jnp.pad(x, ((0, 0), (K - 1, 0), (0, 0)))
            conv = conv_b + sum((xp[:, k:k + L, :] * conv_w[:, k] for k in range(K)))
            x = jax.nn.silu(conv)
            delta = jax.nn.softplus(jnp.einsum('ble,re->blr', x, wd1) @ wd2.T + wd2_b)
            Bt = jnp.einsum('ble,ne->bln', x, wb)
            Ct = jnp.einsum('ble,ne->bln', x, wc)
            A = -jnp.exp(A_log)

            def step(h, inp):
                dt, b_t, c_t, x_t = inp
                A_bar = jnp.exp(dt[:, :, None] * A)
                h = A_bar * h + (dt * x_t)[:, :, None] * b_t[:, None, :]
                y = jnp.einsum('ben,bn->be', h, c_t)
                return (h, y)
            h0 = jnp.zeros((B, E, N), x.dtype)
            xs = (delta.transpose(1, 0, 2), Bt.transpose(1, 0, 2), Ct.transpose(1, 0, 2), x.transpose(1, 0, 2))
            _, y = jax.lax.scan(step, h0, xs)
            y = y.transpose(1, 0, 2)
            y = y + x * W_D
            y = y * jax.nn.silu(skip)
            y = jnp.einsum('ble,de->bld', y, out_w)
            return resid + y
        return _forward(resid, norm_w, skip_w, in_w, conv_w, conv_b, wd1, wd2, wd2_b, wb, wc, A_log, W_D, out_w)

    def _L0_ffn_ref(x, W_fc, W_proj):
        import jax, jax.numpy as jnp
        import numpy as np
        import math
        BETA = 0.9
        THRESHOLD = 1.0
        NUM_STEPS = 5
        ALPHA = 2.0

        @jax.custom_vjp
        def spike_fn(u):
            return (u > 0).astype(u.dtype)

        def _spike_fwd(u):
            return (spike_fn(u), u)

        def _spike_bwd(u, g):
            s = jnp.pi / 2.0 * ALPHA * u
            return (g * (ALPHA / 2.0) / (1.0 + s * s),)
        spike_fn.defvjp(_spike_fwd, _spike_bwd)
        h = jnp.square(jax.nn.relu(jnp.einsum('bsd,fd->bsf', x, W_fc)))
        y = jnp.einsum('bsf,df->bsd', h, W_proj)

        def step(mem, _):
            reset = jax.lax.stop_gradient(spike_fn(mem - THRESHOLD))
            mem_new = BETA * mem + y - reset * THRESHOLD
            spk = spike_fn(mem_new - THRESHOLD)
            return (mem_new, spk)
        mem0 = jnp.zeros_like(y)
        _, spks = jax.lax.scan(step, mem0, None, length=NUM_STEPS)
        return jnp.sum(spks, axis=0) / NUM_STEPS

    def _L1_attn_a_ref(x, gamma, beta, w_qkv, w_out, b_out):
        import jax, jax.numpy as jnp
        import numpy as np
        HEADS = 4
        DIM_HEAD = 32
        EPS = 1e-05
        b, n, dim = x.shape
        mean = jnp.mean(x, axis=2, keepdims=True)
        var = jnp.var(x, axis=2, keepdims=True)
        xn = (x - mean) / jnp.sqrt(var + EPS) * gamma + beta
        qkv = jnp.einsum('bnc,ck->bnk', xn, w_qkv)
        q, k, v = jnp.split(qkv, 3, axis=2)

        def to_heads(t):
            return t.reshape(b, n, HEADS, DIM_HEAD)
        q, k, v = (to_heads(q), to_heads(k), to_heads(v))
        q = q * DIM_HEAD ** (-0.5)
        k = jax.nn.softmax(k, axis=1)
        context = jnp.einsum('bnhd,bnhe->bhde', k, v)
        out = jnp.einsum('bhde,bnhd->bnhe', context, q)
        out = out.reshape(b, n, HEADS * DIM_HEAD)
        out = jnp.einsum('bnk,kc->bnc', out, w_out) + b_out
        return out + x

    def _L1_attn_b_ref(x, w_qkv, b_qkv, w_proj, b_proj):
        import jax, jax.numpy as jnp
        import numpy as np
        HIDDEN = 128
        N_HEADS = 16
        HEAD_DIM = HIDDEN // N_HEADS
        SCALE = HEAD_DIM ** (-0.5)
        b, n, dim = x.shape
        qkv = x @ w_qkv + b_qkv
        qkv = qkv.reshape(b, n, 3, N_HEADS, HEAD_DIM)
        qkv = jnp.transpose(qkv, (2, 0, 3, 1, 4))
        q, k, v = (qkv[0], qkv[1], qkv[2])
        dp = jnp.einsum('bhqd,bhkd->bhqk', q, k) * SCALE
        attn = jax.nn.softmax(dp, axis=1)
        w_avg = jnp.einsum('bhqk,bhkd->bhqd', attn, v)
        w_avg = jnp.transpose(w_avg, (0, 2, 1, 3)).reshape(b, n, dim)
        out = w_avg @ w_proj + b_proj
        return out

    def _L1_ffn_ref(hidden_states, Wg, Wu, Wd):
        import jax, jax.numpy as jnp
        import numpy as np
        NUM_EXPERTS = 8
        HIDDEN = 128
        FFN = 512
        BATCH = 2
        SEQ = 256
        B, S, H = hidden_states.shape
        x = hidden_states.reshape(-1, H)

        def expert_step(acc, w):
            wg, wu, wd = w
            h = jax.nn.silu(x @ wg) * (x @ wu)
            return (acc + h @ wd, None)
        acc, _ = jax.lax.scan(expert_step, jnp.zeros_like(x), (Wg, Wu, Wd))
        return acc.reshape(B, S, H)
    x = L0_attn_a_x_bld
    x = x + _L0_attn_a_ref(_layernorm(x, axis=-1), L0_attn_a_Wq, L0_attn_a_Wkv_down, L0_attn_a_Wk_up, L0_attn_a_Wv_up, L0_attn_a_Wout)
    x = x + _L0_ffn_ref(_layernorm(x, axis=-1), L0_ffn_W_fc, L0_ffn_W_proj)
    x = x + _L0_attn_b_ref(_layernorm(x, axis=-1), L0_attn_b_norm_w, L0_attn_b_skip_w, L0_attn_b_in_w, L0_attn_b_conv_w, L0_attn_b_conv_b, L0_attn_b_wd1, L0_attn_b_wd2, L0_attn_b_wd2_b, L0_attn_b_wb, L0_attn_b_wc, L0_attn_b_A_log, L0_attn_b_W_D, L0_attn_b_out_w)
    x = x + _L0_ffn_ref(_layernorm(x, axis=-1), L0_ffn_W_fc, L0_ffn_W_proj)
    x = x + _L1_attn_a_ref(_layernorm(x, axis=-1), L1_attn_a_gamma, L1_attn_a_beta, L1_attn_a_w_qkv, L1_attn_a_w_out, L1_attn_a_b_out)
    x = x + _L1_ffn_ref(_layernorm(x, axis=-1), L1_ffn_Wg, L1_ffn_Wu, L1_ffn_Wd)
    x = x + _L1_attn_b_ref(_layernorm(x, axis=-1), L1_attn_b_w_qkv, L1_attn_b_b_qkv, L1_attn_b_w_proj, L1_attn_b_b_proj)
    x = x + _L1_ffn_ref(_layernorm(x, axis=-1), L1_ffn_Wg, L1_ffn_Wu, L1_ffn_Wd)
    return x

_drawn_inputs = setup_inputs


def setup_inputs(seed=0):
    import zlib

    import numpy as np

    out = dict(_drawn_inputs(seed))
    spreads = {'L0_attn_b_norm_w': (1.0, 0.2),
     'L0_attn_b_W_D': (1.0, 0.2),
     'L1_attn_a_gamma': (1.0, 0.2),
     'L1_attn_a_beta': (0.0, 0.1),
     'L1_attn_a_b_out': (0.0, 0.1),
     'L1_attn_b_b_qkv': (0.0, 0.1),
     'L1_attn_b_b_proj': (0.0, 0.8)}
    factors = {'L0_attn_b_wd2_b': 4.346}
    for name, (base, spread) in spreads.items():
        noise = np.random.default_rng([zlib.crc32(name.encode()), seed]).standard_normal(out[name].shape)
        drawn = base * np.exp(spread * noise) if base else spread * noise
        out[name] = jnp.asarray(drawn.astype(out[name].dtype))
    for name, factor in factors.items():
        out[name] = (out[name] * factor).astype(out[name].dtype)
    return out
```

```python
from contextlib import ExitStack

import numpy as np

import concourse.bass as bass
from concourse import mybir

ALU = mybir.AluOpType
ACT = mybir.ActivationFunctionType
AX = mybir.AxisListType.X
F32 = mybir.dt.float32
F32R = mybir.dt.float32r
BF16 = mybir.dt.bfloat16

P = 128
B, L, D = 2, 1024, 128
T = B * L
NB = T // P
LB = L // P
EPS = 1e-5
MASKED = -3.0e38
AF_WORDS, AR_WORDS = 21 * 1024, 15616


def wait(eng, sem, n):
    if n > 0:
        eng.wait_ge(sem, n)


class Chain:

    def __init__(self, eng, sem):
        self.eng, self.sem, self.n = eng, sem, 0

    def __call__(self, ins):
        self.n += 1
        ins.then_inc(self.sem, 1)
        self.eng.wait_ge(self.sem, self.n)


def mm3(pe, out, lhs, rhs, start=True, stop=True):
    (ah, al), (bh, bl) = lhs, rhs
    pe.matmul(out, ah, bh, start=start, stop=False)
    pe.matmul(out, ah, bl, start=False, stop=False)
    return pe.matmul(out, al, bh, start=False, stop=stop)


def f32(ap):
    return ap.bitcast(F32)


def build(nc, a, out, upto=8):
    ctx = ExitStack()
    with ctx:
        def sb(name, shape, dt=F32):
            return ctx.enter_context(nc.sbuf_tensor(name, shape, dt))

        def sem(name):
            return ctx.enter_context(nc.semaphore(name))

        ps = ctx.enter_context(nc.psum_tensor("ps", [P, 8, 512], F32))

        def bank(i, n=1):
            return ps[:, i:i + n, :].rearrange("p b c -> p (b c)")

        ident = sb("ident", [P, P])
        ident_bf = sb("ident_bf", [P, P], BF16)
        causal_bf = sb("causal_bf", [P, P], BF16)
        half_pow = sb("half_pow", [P, NB])
        ones_row = sb("ones_row", [1, P])
        X = sb("X", [P, NB, D])
        R = sb("R", [P, NB, D])
        XN = sb("XN", [P, NB, D])
        XH = sb("XH", [P, T], F32R)
        XL = sb("XL", [P, T], F32R)
        stats = sb("stats", [P, NB, 6])
        mv = sb("mv", [P, NB, 2])
        var_eps = sb("var_eps", [P, NB])
        rstd = sb("rstd", [P, NB])
        gain = sb("gain", [P, 3])
        lnt = sb("lnt", [P, 2, 512])
        AF = sb("AF", [P, AF_WORDS])
        AR = sb("AR", [P, AR_WORDS], F32R)

        def carver(arena, total):
            at = [0]

            def take(*shape):
                n = 1
                for s in shape:
                    n *= s
                lo = at[0]
                at[0] += n
                assert at[0] <= total, (at[0], total)
                v = arena[:, lo:lo + n]
                if len(shape) == 2:
                    v = v.rearrange("p (a b) -> p a b", a=shape[0])
                if len(shape) == 3:
                    v = v.rearrange("p (a b c) -> p a b c", a=shape[0], b=shape[1])
                return v
            return take

        chain_dve = sem("chain_dve")
        chain_act = sem("chain_act")
        chain_pool = sem("chain_pool")
        consts_ready = sem("consts_ready")
        x_loaded = sem("x_loaded")
        ln_stat = sem("ln_stat")
        ln_rstd = sem("ln_rstd")
        ln_norm = sem("ln_norm")
        ln_tr = sem("ln_tr")
        ln_hi = sem("ln_hi")
        ln_lo = sem("ln_lo")
        x_done = sem("x_done")
        out_sem = sem("out_sem")

        x_dram = a["L0_attn_a_x_bld"].rearrange("b (n p) d -> p (b n) d", p=P)
        out_dram = out.rearrange("b (n p) d -> p (b n) d", p=P)

        DOUBLE = (2, 4)

        def rounds(s):
            return s + sum(1 for k in DOUBLE if k < s)

        def ln_dve(dve, link, s, per_batch=None):
            def stat(src, r):
                for t in range(NB):
                    dve.bn_stats(stats[:, t, :], src[:, t, :]).then_inc(chain_dve, 1)
                    link.n += 1
                dve.wait_ge(chain_dve, link.n)
                for t in range(NB):
                    ins = dve.bn_aggr(mv[:, t, :], stats[:, t, :])
                    ins.then_inc(ln_stat, 1)
                dve.wait_ge(ln_stat, NB * (r + 1))
                dve.wait_ge(ln_rstd, r + 1)
            r = rounds(s)
            if s == 0:
                dve.wait_ge(x_loaded, 16)
            stat(X, r)
            for t in range(NB):
                dve.tensor_scalar(R[:, t, :], X[:, t, :], mv[:, t, 0:1], rstd[:, t:t + 1],
                                  ALU.subtract, ALU.mult).then_inc(ln_norm if s not in DOUBLE else chain_dve, 1)
                if s in DOUBLE:
                    link.n += 1
            if s in DOUBLE:
                dve.wait_ge(chain_dve, link.n)
                stat(R, r + 1)
                for t in range(NB):
                    if s == 4:
                        ins = dve.tensor_scalar(XN[:, t, :], R[:, t, :], mv[:, t, 0:1], rstd[:, t:t + 1],
                                                ALU.subtract, ALU.mult)
                    else:
                        ins = dve.tensor_scalar(XN[:, t, :], R[:, t, :], rstd[:, t:t + 1], None, ALU.mult)
                    ins.then_inc(ln_norm, 1)
            for i in range(4):
                dve.wait_ge(ln_hi, 4 * s + i + 1)
                src = lnt[:, i % 2, :] if s in DOUBLE else bank(i % 2)
                dve.tensor_tensor(XL[:, 512 * i:512 * i + 512], src, f32(XH[:, 512 * i:512 * i + 512]),
                                  ALU.subtract).then_inc(ln_lo, 1)

        def ln_pool(pool, link, s):
            for k in range(2 if s in DOUBLE else 1):
                r = rounds(s) + k
                pool.wait_ge(ln_stat, NB * (r + 1))
                if s == 2 and k == 1:
                    link(pool.tensor_tensor(var_eps[:, :], mv[:, :, 0], mv[:, :, 0], ALU.mult))
                    link(pool.tensor_tensor(var_eps[:, :], var_eps[:, :], mv[:, :, 1], ALU.add))
                    link(pool.tensor_scalar(var_eps[:, :], var_eps[:, :], EPS, None, ALU.add))
                else:
                    link(pool.tensor_scalar(var_eps[:, :], mv[:, :, 1], EPS, None, ALU.add))
                pool.tensor_tensor(rstd[:, :], var_eps[:, :], half_pow[:, :], ALU.pow).then_inc(ln_rstd, 1)

        def ln_pe(pe, s):
            src = XN if s in DOUBLE else R
            for i in range(4):
                pe.wait_ge(ln_norm, NB * s + 4 * i + 4)
                if i >= 2:
                    pe.wait_ge(ln_lo, 4 * s + i - 1)
                for j in range(4):
                    ins = pe.transpose(bank(i % 2)[:, P * j:P * j + P], src[:, 4 * i + j, :], ident[:, :])
                ins.then_inc(ln_tr, 1)

        def ln_act(act, link, s):
            for i in range(4):
                act.wait_ge(ln_tr, 4 * s + i + 1)
                hi = XH[:, 512 * i:512 * i + 512]
                if s in DOUBLE:
                    if i >= 2:
                        act.wait_ge(ln_lo, 4 * s + i - 1)
                    g = gain[:, 0:1] if s == 2 else gain[:, 1:2]
                    b = 0.0 if s == 2 else gain[:, 2:3]
                    link(act.activation(lnt[:, i % 2, :], bank(i % 2), ACT.Identity, scale=g, bias=b))
                    act.activation(hi, lnt[:, i % 2, :], ACT.Copy).then_inc(ln_hi, 1)
                else:
                    act.activation(hi, bank(i % 2), ACT.Copy).then_inc(ln_hi, 1)

        def xt(lo, n):
            return XH[:, lo:lo + n], XL[:, lo:lo + n]

        H0, HD, LD = 16, 64, 32
        G0 = H0 // 4
        tf, tr = carver(AF, AF_WORDS), carver(AR, AR_WORDS)
        wq_raw = tf(H0 * HD)
        wkup_raw = tf(H0 * HD)
        wvup_raw = tf(H0 * HD)
        wout_raw = tf(8, D)
        wkv_raw = tf(LD)
        wqT = tf(H0 * HD)
        wkT = tf(8, LD)
        wvT = tf(8, LD)
        a32 = tf(H0, LD)
        bcomb = tf(G0, D)
        lat_tok = tf(LB, LD)
        rinv_x = tf(LB, P)
        rb = tf(L)
        ot = tf(G0, L)
        pm = tf(2, L)
        pt = tf(4, 512)
        negm = tf(4)
        rsum = tf(4)
        rinv = tf(LB, 4)
        arep = [tr(H0, P), tr(H0, P)]
        wkv4 = [tr(P), tr(P)]
        kst = tr(L)
        qst = tr(4, L)

        s0_w = sem("s0_w")
        s0_wT = sem("s0_wT")
        s0_wTc = sem("s0_wTc")
        s0_ab = sem("s0_ab")
        s0_ahi = sem("s0_ahi")
        s0_alo = sem("s0_alo")
        s0_lat = sem("s0_lat")
        s0_khi = sem("s0_khi")
        s0_klo = sem("s0_klo")
        s0_latc = sem("s0_latc")
        s0_q = sem("s0_q")
        s0_qhi = sem("s0_qhi")
        s0_qlo = sem("s0_qlo")
        s0_s = sem("s0_s")
        s0_m = sem("s0_m")
        s0_e = sem("s0_e")
        s0_ri = sem("s0_ri")
        s0_t = sem("s0_t")
        s0_ca = sem("s0_ca")
        s0_cd = sem("s0_cd")
        s0_pv = sem("s0_pv")
        s0_rx = sem("s0_rx")
        s0_rp = sem("s0_rp")
        s0_rc = sem("s0_rc")
        s0_ot = sem("s0_ot")
        s0_y = sem("s0_y")

        STEPS = [(hh, qb) for hh in range(4) for qb in range(LB)]
        CH = [(u, c, min(4, qb + 1 - 4 * c)) for u, (hh, qb) in enumerate(STEPS) for c in range((qb + 4) // 4)]
        FIRST_CH = [next(i for i, x in enumerate(CH) if x[0] == u) for u in range(len(STEPS))] + [len(CH)]
        NU, NC = len(STEPS), len(CH)

        def on_dve(i):
            return i % 3 == 0

        def copies(i, dve):
            full, rest = divmod(i, NC)
            per = sum(1 for k in range(NC) if on_dve(k) == dve)
            return full * per + sum(1 for k in range(rest) if on_dve(k) == dve)

        def copied(eng, n):
            wait(eng, s0_cd, copies(n, True))
            wait(eng, s0_ca, copies(n, False))

        def s0_load(q):
            q.dma_start(wq_raw, a["L0_attn_a_Wq"].rearrange("d h k -> d (h k)")).then_inc(s0_w, 16)
            q.dma_start(wkup_raw[0:LD], a["L0_attn_a_Wk_up"].rearrange("d h k -> d (h k)")).then_inc(s0_w, 16)
            q.dma_start(wvup_raw[0:LD], a["L0_attn_a_Wv_up"].rearrange("d h k -> d (h k)")).then_inc(s0_w, 16)
            q.dma_start(wout_raw, a["L0_attn_a_Wout"].rearrange("(j h) k o -> (h k) j o", h=2)).then_inc(s0_w, 16)
            q.dma_start(wkv_raw, a["L0_attn_a_Wkv_down"]).then_inc(s0_w, 16)

        def s0_pe(pe):
            pe.wait_ge(s0_w, 80)
            pe.wait_ge(consts_ready, 1)
            for j in range(8):
                pe.transpose(bank(2 + j // 4)[:, P * (j % 4):P * (j % 4) + P], wq_raw[:, P * j:P * j + P], ident[:, :])
                pe.transpose(bank(4)[:, LD * j:LD * j + LD], wkup_raw[0:LD, P * j:P * j + P], ident[0:LD, 0:LD])
                ins = pe.transpose(bank(4)[:, 256 + LD * j:256 + LD * j + LD], wvup_raw[0:LD, P * j:P * j + P],
                                   ident[0:LD, 0:LD])
            ins.then_inc(s0_wT, 1)
            pe.wait_ge(s0_wTc, 3)
            for h in range(H0):
                r, j = 64 * (h % 2), h // 2
                pe.matmul(bank(5 + 2 * (h % 2))[:, LD * j:LD * j + LD], wqT[r:r + 64, P * j:P * j + P], wkT[r:r + 64, j, :],
                          start=True, stop=True)
            for h in range(H0):
                r, j, c = 64 * (h % 2), h // 2, LD * (h % 4)
                ins = pe.matmul(bank(6 if h % 2 == 0 else 2)[c:c + LD, P * (h // 4):P * (h // 4) + P], wvT[r:r + 64, j, :],
                                wout_raw[r:r + 64, j, :], start=True, stop=True)
            ins.then_inc(s0_ab, 1)
            ln_pe(pe, 0)
            pe.wait_ge(s0_alo, 2)
            for b in range(B):
                if b:
                    pe.wait_ge(x_done, b)
                for i in range(2):
                    pe.wait_ge(ln_lo, 2 * b + i + 1)
                    mm3(pe, bank(2 + i), (wkv4[0], wkv4[1]), xt(L * b + 512 * i, 512)).then_inc(s0_lat, 1)
                for t in range(LB):
                    ins = mm3(pe, bank(4)[:, LD * t:LD * t + LD], xt(L * b + P * t, P),
                              (wkv4[0][:, 0:LD], wkv4[1][:, 0:LD]))
                ins.then_inc(s0_lat, 1)
                pe.wait_ge(s0_klo, 2 * b + 2)
                pe.wait_ge(s0_latc, b + 1)
                for g in range(G0):
                    gg = b * G0 + g
                    wait(pe, s0_ot, gg)
                    for n in range(8):
                        hh, i = n // 2, n % 2
                        if n >= 4:
                            pe.wait_ge(s0_qlo, 8 * gg + n - 3)
                        mm3(pe, bank(n % 4), (arep[0][:, 4 * g + hh, :], arep[1][:, 4 * g + hh, :]),
                            xt(L * b + 512 * i, 512)).then_inc(s0_q, 1)
                    pe.wait_ge(s0_qlo, 8 * gg + 8)

                    def scores(u):
                        hh, qb = STEPS[u]
                        if u >= 2:
                            pe.wait_ge(s0_e, NU * gg + u - 1)
                        for c in range((qb + 4) // 4):
                            n = min(4, qb + 1 - 4 * c) * P
                            o = bank(2 * (u % 2) + c)
                            pe.matmul(o[:, 0:n], qst[:, hh, P * qb:P * qb + P], kst[:, 512 * c:512 * c + n],
                                      start=True, stop=True)
                        pe.matmul(o[:, n - P:n], ident_bf[:, :], causal_bf[:, :], start=False, stop=True,
                                  skip_group_check=True).then_inc(s0_s, 1)

                    def turn(u):
                        pe.wait_ge(s0_e, NU * gg + u + 1)
                        for i in range(FIRST_CH[u], FIRST_CH[u + 1]):
                            _, c, n = CH[i]
                            k = NC * gg + i
                            copied(pe, k - 1)
                            for j in range(n):
                                ins = pe.transpose(bank(4 + k % 2)[:, P * j:P * j + P],
                                                   pm[:, u % 2, P * (4 * c + j):P * (4 * c + j) + P], ident[:, :])
                            ins.then_inc(s0_t, 1)

                    def pv(u):
                        hh, qb = STEPS[u]
                        for i in range(FIRST_CH[u], FIRST_CH[u + 1]):
                            _, c, n = CH[i]
                            k = NC * gg + i
                            copied(pe, k + 1)
                            for j in range(n):
                                kb = 4 * c + j
                                ins = pe.matmul(bank(6 + qb // 4)[LD * hh:LD * hh + LD, P * (qb % 4):P * (qb % 4) + P],
                                                lat_tok[:, kb, :], pt[:, k % 4, P * j:P * j + P],
                                                start=kb == 0, stop=kb == qb)
                            ins.then_inc(s0_pv, 1)

                    scores(0)
                    for u in range(NU):
                        if u + 1 < NU:
                            scores(u + 1)
                        turn(u)
                        if u:
                            pv(u - 1)
                    pv(NU - 1)
                    pe.wait_ge(s0_rx, gg + 1)
                    for qb in range(LB):
                        ins = pe.matmul(bank(qb // 4)[:, P * (qb % 4):P * (qb % 4) + P], rinv_x[:, qb, :],
                                        ident[:, :], start=True, stop=True)
                    ins.then_inc(s0_rp, 1)
                pe.wait_ge(s0_ot, G0 * (b + 1))
                for t in range(LB):
                    for g in range(G0):
                        ins = pe.matmul(bank(2 + t // 4)[:, P * (t % 4):P * (t % 4) + P], ot[:, g, P * t:P * t + P],
                                        bcomb[:, g, :], start=g == 0, stop=g == G0 - 1)
                ins.then_inc(s0_y, 1)

        def s0_act(act, link):
            act.wait_ge(s0_wT, 1)
            act.activation(wqT, bank(2, 2), ACT.Copy).then_inc(s0_wTc, 1)
            act.activation(wkT, bank(4)[:, 0:256].rearrange("p (j c) -> p j c", j=8), ACT.Copy).then_inc(s0_wTc, 1)
            act.activation(wvT, bank(4)[:, 256:512].rearrange("p (j c) -> p j c", j=8), ACT.Copy).then_inc(s0_wTc, 1)
            act.wait_ge(s0_ab, 1)
            for r in range(2):
                act.activation(a32.rearrange("p (j r) c -> p j r c", r=2)[:, :, r, :],
                               bank(5 + 2 * r)[:, 0:256].rearrange("p (j c) -> p j c", j=8), ACT.Copy,
                               scale=HD ** -0.5).then_inc(chain_act, 1)
                link.n += 1
            for h in range(4):
                c = LD * h
                act.activation(bcomb[c:c + LD], bank(6 if h % 2 == 0 else 2)[c:c + LD].rearrange(
                    "p (g o) -> p g o", g=G0), ACT.Copy).then_inc(chain_act, 1)
                link.n += 1
            act.wait_ge(chain_act, link.n)
            act.activation(arep[0].rearrange("p h (r c) -> p h r c", r=4),
                           a32.unsqueeze(2).to_broadcast([P, H0, 4, LD]), ACT.Copy).then_inc(s0_ahi, 1)
            act.activation(wkv4[0].rearrange("p (r c) -> p r c", r=4),
                           wkv_raw.unsqueeze(1).to_broadcast([P, 4, LD]), ACT.Copy).then_inc(s0_ahi, 1)
            ln_act(act, link, 0)
            for b in range(B):
                for i in range(2):
                    act.wait_ge(s0_lat, 3 * b + i + 1)
                    act.activation(kst[:, 512 * i:512 * i + 512], bank(2 + i), ACT.Copy).then_inc(s0_khi, 1)
                act.wait_ge(s0_lat, 3 * b + 3)
                act.activation(lat_tok, bank(4)[:, 0:LB * LD].rearrange("p (t c) -> p t c", t=LB),
                               ACT.Copy).then_inc(s0_latc, 1)
                for g in range(G0):
                    gg = b * G0 + g
                    for n in range(8):
                        act.wait_ge(s0_q, 8 * gg + n + 1)
                        act.activation(qst[:, n // 2, 512 * (n % 2):512 * (n % 2) + 512], bank(n % 4),
                                       ACT.Copy).then_inc(s0_qhi, 1)

                    def copy_chunks(u):
                        for i in range(FIRST_CH[u], FIRST_CH[u + 1]):
                            if on_dve(i):
                                continue
                            k, n = NC * gg + i, CH[i][2] * P
                            act.wait_ge(s0_t, k + 1)
                            wait(act, s0_pv, k - 3)
                            act.activation(pt[:, k % 4, 0:n], bank(4 + k % 2)[:, 0:n], ACT.Copy).then_inc(s0_ca, 1)

                    for u, (hh, qb) in enumerate(STEPS):
                        n = (qb + 1) * P
                        act.wait_ge(s0_m, NU * gg + u + 1)
                        if u >= 2:
                            act.wait_ge(s0_t, NC * gg + FIRST_CH[u - 1])
                        if NU * gg + u >= 4:
                            act.wait_ge(s0_ri, NU * gg + u - 3)
                        act.activation(pm[:, u % 2, 0:n], bank(2 * (u % 2), 2)[:, 0:n], ACT.Exp,
                                       bias=negm[:, u % 4:u % 4 + 1],
                                       accum_out=rsum[:, u % 4:u % 4 + 1]).then_inc(s0_e, 1)
                        if u:
                            copy_chunks(u - 1)
                    copy_chunks(NU - 1)
                    act.wait_ge(s0_ri, NU * gg + NU)
                    act.activation(rinv_x.rearrange("p t (h c) -> p t h c", h=4),
                                   rinv.unsqueeze(3).to_broadcast([P, LB, 4, LD]), ACT.Copy).then_inc(s0_rx, 1)
                    act.wait_ge(s0_rp, gg + 1)
                    act.activation(rb, bank(0, 2), ACT.Copy).then_inc(s0_rc, 1)

        def s0_dve(dve, link):
            dve.wait_ge(s0_ahi, 2)
            dve.tensor_tensor(arep[1].rearrange("p h (r c) -> p h r c", r=4),
                              a32.unsqueeze(2).to_broadcast([P, H0, 4, LD]),
                              f32(arep[0]).rearrange("p h (r c) -> p h r c", r=4), ALU.subtract).then_inc(s0_alo, 1)
            dve.tensor_tensor(wkv4[1].rearrange("p (r c) -> p r c", r=4),
                              wkv_raw.unsqueeze(1).to_broadcast([P, 4, LD]),
                              f32(wkv4[0]).rearrange("p (r c) -> p r c", r=4), ALU.subtract).then_inc(s0_alo, 1)
            ln_dve(dve, link, 0)
            for b in range(B):
                for i in range(2):
                    dve.wait_ge(s0_khi, 2 * b + i + 1)
                    for r in (32, 96):
                        k = kst[r:r + 32, 512 * i:512 * i + 512]
                        ins = dve.tensor_tensor(k, bank(2 + i)[r:r + 32], f32(k), ALU.subtract)
                    ins.then_inc(s0_klo, 1)
                for g in range(G0):
                    gg = b * G0 + g
                    for n in range(8):
                        dve.wait_ge(s0_qhi, 8 * gg + n + 1)
                        q = qst[64:128, n // 2, 512 * (n % 2):512 * (n % 2) + 512]
                        dve.tensor_tensor(q, bank(n % 4)[64:128], f32(q), ALU.subtract).then_inc(s0_qlo, 1)

                    def finish(u):
                        hh, qb = STEPS[u]
                        dve.wait_ge(s0_e, NU * gg + u + 1)
                        dve.reciprocal(rinv[:, qb, hh:hh + 1], rsum[:, u % 4:u % 4 + 1]).then_inc(s0_ri, 1)
                        for i in range(FIRST_CH[u], FIRST_CH[u + 1]):
                            if not on_dve(i):
                                continue
                            k, n = NC * gg + i, CH[i][2] * P
                            dve.wait_ge(s0_t, k + 1)
                            wait(dve, s0_pv, k - 3)
                            dve.tensor_copy(pt[:, k % 4, 0:n], bank(4 + k % 2)[:, 0:n]).then_inc(s0_cd, 1)

                    if gg:
                        dve.wait_ge(s0_rx, gg)
                    for u, (hh, qb) in enumerate(STEPS):
                        n = (qb + 1) * P
                        dve.wait_ge(s0_s, NU * gg + u + 1)
                        if u >= 4 or gg:
                            dve.wait_ge(s0_e, NU * gg + u - 3)
                        dve.tensor_reduce(negm[:, u % 4:u % 4 + 1], bank(2 * (u % 2), 2)[:, 0:n], AX, ALU.max,
                                          negate=True).then_inc(s0_m, 1)
                        if u:
                            finish(u - 1)
                    finish(NU - 1)
                    dve.wait_ge(s0_rc, gg + 1)
                    dve.wait_ge(s0_pv, NC * (gg + 1))
                    wait(dve, s0_y, b)
                    dve.tensor_tensor(ot[:, g, :], bank(6, 2), rb, ALU.mult).then_inc(s0_ot, 1)
                dve.wait_ge(s0_y, b + 1)
                xb = X[:, LB * b:LB * b + LB, :].rearrange("p t d -> p (t d)")
                ins = dve.tensor_tensor(xb, xb, bank(2, 2), ALU.add).then_inc(x_done, 1)
                dve.wait_ge(x_done, b + 1)

        FF = 4
        tf, tr = carver(AF, AF_WORDS), carver(AR, AR_WORDS)
        wfc_raw = tf(FF, D)
        wpj_raw = tf(FF * P)
        wpjT = tf(FF, D)
        ffr = tf(2, 512)
        ffh = tf(2, FF, 512)
        cnt = tf(2, 512)
        yv = tf(2, 512)
        fcT = [tr(FF * P), tr(FF * P)]

        def spike_thresholds(steps=5, beta=0.9, threshold=1.0):
            f = np.float32

            def spikes(y):
                mem, n = f(0), 0
                for _ in range(steps):
                    reset = f(1) if mem - f(threshold) > 0 else f(0)
                    mem = f(f(f(beta) * mem) + y) - reset * f(threshold)
                    n += int(mem - f(threshold) > 0)
                return n
            found = []
            for k in range(1, steps + 1):
                lo, hi = f(0), f(4)
                while np.nextafter(lo, hi) < hi:
                    mid = f((lo + hi) / f(2))
                    lo, hi = (lo, mid) if spikes(mid) >= k else (mid, hi)
                found.append(float(lo))
            return found

        THR = spike_thresholds()

        s1_w = sem("s1_w")
        s1_wT = sem("s1_wT")
        s1_fhi = sem("s1_fhi")
        s1_flo = sem("s1_flo")
        s1_z = sem("s1_z")
        s1_r = sem("s1_r")
        s1_h = sem("s1_h")
        s1_y = sem("s1_y")
        s1_yc = sem("s1_yc")

        def s1_load(q, s):
            q.wait_ge(x_done, X_AFTER[s])
            q.dma_start(wfc_raw, a["L0_ffn_W_fc"].rearrange("(c p) d -> p c d", p=P)).then_inc(s1_w, 16)
            q.dma_start(wpj_raw, a["L0_ffn_W_proj"]).then_inc(s1_w, 16)

        def s1_pe(pe, s):
            k = s // 2
            pe.wait_ge(s1_w, 32 * (k + 1))
            for c in range(FF):
                pe.transpose(bank(2)[:, P * c:P * c + P], wfc_raw[:, c, :], ident[:, :])
            for c in range(FF):
                ins = pe.transpose(bank(3)[:, P * c:P * c + P], wpj_raw[:, P * c:P * c + P], ident[:, :])
            ins.then_inc(s1_wT, 1)
            ln_pe(pe, s)
            pe.wait_ge(s1_flo, k + 1)
            for i in range(4):
                pe.wait_ge(ln_lo, 4 * s + i + 1)
                for c in range(FF):
                    n = 16 * k + 4 * i + c
                    wait(pe, s1_h, n - 1)
                    mm3(pe, bank(2 + n % 2), (fcT[0][:, P * c:P * c + P], fcT[1][:, P * c:P * c + P]),
                        xt(512 * i, 512)).then_inc(s1_z, 1)
                if i:
                    down(pe, k, i - 1)
            down(pe, k, 3)

        def down(pe, k, i):
            n = 4 * k + i
            pe.wait_ge(s1_h, 16 * k + 4 * i + 4)
            wait(pe, s1_yc, n - 1)
            for t in range(4):
                for c in range(FF):
                    ins = pe.matmul(bank(4 + n % 2)[:, P * t:P * t + P], ffh[:, i % 2, c, P * t:P * t + P],
                                    wpjT[:, c, :], start=c == 0, stop=c == FF - 1)
            ins.then_inc(s1_y, 1)

        def s1_act(act, link, s):
            k = s // 2
            act.wait_ge(s1_wT, k + 1)
            act.activation(fcT[0], bank(2), ACT.Copy).then_inc(s1_fhi, 1)
            link(act.activation(wpjT, bank(3).rearrange("p (c d) -> p c d", c=FF), ACT.Copy))
            ln_act(act, link, s)
            for n in range(16 * k, 16 * k + 16):
                act.wait_ge(s1_z, n + 1)
                wait(act, s1_h, n - 1)
                act.activation(ffr[:, n % 2, :], bank(2 + n % 2), ACT.Relu).then_inc(s1_r, 1)

        def s1_dve(dve, link, s):
            k = s // 2
            dve.wait_ge(s1_fhi, k + 1)
            dve.tensor_tensor(fcT[1], bank(2), f32(fcT[0]), ALU.subtract).then_inc(s1_flo, 1)
            ln_dve(dve, link, s)

            def spikes(i):
                n = 4 * k + i
                dve.wait_ge(s1_y, n + 1)
                y, c = yv[:, i % 2, :], cnt[:, i % 2, :]
                dve.tensor_copy(y, bank(4 + n % 2)).then_inc(s1_yc, 1)
                dve.wait_ge(s1_yc, n + 1)
                link(dve.tensor_scalar(c, y, THR[0], None, ALU.is_gt))
                for thr in THR[1:]:
                    link(dve.scalar_tensor_tensor(out=c, in0=y, scalar=thr, in1=c, op0=ALU.is_gt, op1=ALU.add))
                xs = X[:, 4 * i:4 * i + 4, :].rearrange("p t d -> p (t d)")
                dve.scalar_tensor_tensor(out=xs, in0=c, scalar=1.0 / len(THR), in1=xs, op0=ALU.mult,
                                         op1=ALU.add).then_inc(x_done, 1)

            for i in range(4):
                for c in range(FF):
                    n = 16 * k + 4 * i + c
                    dve.wait_ge(s1_r, n + 1)
                    if i >= 2:
                        dve.wait_ge(s1_y, 4 * k + i - 1)
                    dve.scalar_tensor_tensor(out=ffh[:, i % 2, c, :], in0=bank(2 + n % 2), scalar=0.0,
                                             in1=ffr[:, n % 2, :], op0=ALU.max, op1=ALU.mult).then_inc(s1_h, 1)
                if i:
                    spikes(i - 1)
            spikes(3)
            dve.wait_ge(x_done, X_AFTER[s + 1])

        NE, FE = 8, 4
        tf, tr = carver(AF, AF_WORDS), carver(AR, AR_WORDS)
        WCOL = 3 * FE * P
        mraw = tf(2, WCOL)
        msg = tf(2, 512)
        mh = tf(2, 512)
        macc = tf(4, 512)
        mwh = [tr(WCOL), tr(WCOL)]
        mwl = [tr(WCOL), tr(WCOL)]
        mhh = tr(2, 512)
        mhl = tr(2, 512)

        m_w = sem("m_w")
        m_w2 = sem("m_w2")
        m_wh = sem("m_wh")
        m_wl = sem("m_wl")
        m_gu = sem("m_gu")
        m_sg = sem("m_sg")
        m_h = sem("m_h")
        m_hh = sem("m_hh")
        m_hl = sem("m_hl")
        m_d = sem("m_d")
        m_y = sem("m_y")
        m_acc = sem("m_acc")
        m_tr = sem("m_tr")

        NT = 4
        PER = NE * NT * FE

        def moe_load(q, s):
            k = (s - 5) // 2
            q.wait_ge(x_done, X_AFTER[s])
            for e in range(NE):
                n = NE * k + e
                wait(q, m_wl, n - 1)
                w = mraw[:, n % 2, :]
                r = (m_w, m_w2)[n % 2]
                q.dma_start(w[:, 0:512], a["L1_ffn_Wg"][e]).then_inc(r, 16)
                q.dma_start(w[:, 512:1024], a["L1_ffn_Wu"][e]).then_inc(r, 16)
                q.dma_start(w[:, 1024:WCOL].rearrange("p (c d) -> p c d", c=FE),
                            a["L1_ffn_Wd"][e].rearrange("(c p) d -> p c d", p=P)).then_inc(r, 16)

        def moe_weights(n):
            return mwh[n % 2], mwl[n % 2]

        def moe_pe(pe, s):
            k = (s - 5) // 2
            ln_pe(pe, s)

            def up(n):
                e, i, c = n // (NT * FE), n // FE % NT, n % FE
                m = PER * k + n
                if n % (NT * FE) == 0:
                    pe.wait_ge(m_wl, NE * k + e + 1)
                pe.wait_ge(ln_lo, 4 * s + i + 1)
                wait(pe, m_h, m - 1)
                wh, wl = moe_weights(NE * k + e)
                for g in range(2):
                    o = 512 * g + P * c
                    ins = mm3(pe, bank(2 * g + m % 2), (wh[:, o:o + P], wl[:, o:o + P]), xt(512 * i, 512))
                ins.then_inc(m_gu, 1)

            def down_e(n):
                e, i, c = n // (NT * FE), n // FE % NT, n % FE
                m = PER * k + n
                pe.wait_ge(m_hl, m + 1)
                wh, wl = moe_weights(NE * k + e)
                o = 1024 + P * c
                if c == 0:
                    wait(pe, m_acc, m // FE - 1)
                mm3(pe, bank(4 + m // FE % 2), (wh[:, o:o + P], wl[:, o:o + P]),
                    (mhh[:, m % 2, :], mhl[:, m % 2, :]), start=c == 0, stop=c == FE - 1).then_inc(m_d, 1)

            pe.wait_ge(ln_lo, 4 * s + 4)
            up(0)
            for n in range(PER):
                if n + 1 < PER:
                    up(n + 1)
                down_e(n)
            for i in range(NT):
                pe.wait_ge(m_acc, NE * NT * (k + 1) - NT + i + 1)
                for t in range(4):
                    ins = pe.transpose(bank(6 + i % 2)[:, P * t:P * t + P], macc[:, i, P * t:P * t + P], ident[:, :])
                ins.then_inc(m_tr, 1)
                if i == 1:
                    pe.wait_ge(x_done, X_AFTER[s] + 2)

        def moe_act(act, link, s):
            k = (s - 5) // 2

            def split(n):
                act.wait_ge((m_w, m_w2)[n % 2], 48 * (n // 2 + 1))
                wait(act, m_d, NT * FE * (n - 1))
                act.activation(mwh[n % 2], mraw[:, n % 2, :], ACT.Copy).then_inc(m_wh, 1)

            split(NE * k)
            ln_act(act, link, s)
            for n in range(PER):
                m = PER * k + n
                act.wait_ge(m_gu, m + 1)
                wait(act, m_h, m - 1)
                act.activation(msg[:, m % 2, :], bank(m % 2), ACT.Silu).then_inc(m_sg, 1)
                if n:
                    hi(act, m - 1)
                if n % (NT * FE) == 2 and n // (NT * FE) + 1 < NE:
                    split(NE * k + n // (NT * FE) + 1)
            hi(act, PER * k + PER - 1)

        def hi(act, m):
            act.wait_ge(m_h, m + 1)
            wait(act, m_d, m - 1)
            act.activation(mhh[:, m % 2, :], mh[:, m % 2, :], ACT.Copy).then_inc(m_hh, 1)

        def moe_dve(dve, link, s):
            k = (s - 5) // 2

            def split(n):
                dve.wait_ge(m_wh, n + 1)
                dve.tensor_tensor(mwl[n % 2], mraw[:, n % 2, :], f32(mwh[n % 2]), ALU.subtract).then_inc(m_wl, 1)

            def finish(n):
                m = PER * k + n
                dve.wait_ge(m_hh, m + 1)
                dve.tensor_tensor(mhl[:, m % 2, :], mh[:, m % 2, :], f32(mhh[:, m % 2, :]),
                                  ALU.subtract).then_inc(m_hl, 1)

            def total(q):
                e, i = q // NT, q % NT
                dve.wait_ge(m_d, FE * (NE * NT * k + q + 1))
                o = bank(4 + q % 2)
                if e == 0:
                    dve.tensor_copy(macc[:, i, :], o).then_inc(m_acc, 1)
                else:
                    dve.tensor_tensor(macc[:, i, :], macc[:, i, :], o, ALU.add).then_inc(m_acc, 1)

            split(NE * k)
            ln_dve(dve, link, s)
            for n in range(PER):
                m = PER * k + n
                dve.wait_ge(m_sg, m + 1)
                wait(dve, m_hl, m - 1)
                dve.tensor_tensor(mh[:, m % 2, :], bank(2 + m % 2), msg[:, m % 2, :], ALU.mult).then_inc(m_h, 1)
                if n:
                    finish(n - 1)
                if n % FE == 2 and n > FE:
                    total(n // FE - 1)
                if n % (NT * FE) == 3 and n // (NT * FE) + 1 < NE:
                    split(NE * k + n // (NT * FE) + 1)
            finish(PER - 1)
            total(NE * NT - 1)
            for i in range(NT):
                dve.wait_ge(m_tr, NT * k + i + 1)
                xs = X[:, 4 * i:4 * i + 4, :].rearrange("p t d -> p (t d)")
                dve.tensor_tensor(xs, xs, bank(6 + i % 2), ALU.add).then_inc(x_done, 1)
            dve.wait_ge(x_done, X_AFTER[s + 1])

        E2, NS, DT, KW = 256, 16, 64, 4
        EC = E2 // P
        EG = P // NS
        NG = P // EG
        tf, tr = carver(AF, AF_WORDS), carver(AR, AR_WORDS)
        sw_raw = tf(EC, D)
        iw_raw = tf(EC, D)
        cw = tf(EC, KW)
        cb = tf(EC)
        db = tf(EC)
        wdd = tf(EC)
        wd1_raw = tf(E2)
        wd2_raw = tf(EC, DT)
        wb_raw = tf(E2)
        wc_raw = tf(E2)
        al_raw = tf(P)
        ow_raw = tf(E2)
        wd1T = tf(EC, DT)
        wd2T = tf(E2)
        wbT = tf(EC, P)
        wcT = tf(EC, P)
        negA = tf(EC * NG)
        owT = tf(EC, D)
        gather = tf(4, 32)
        xp = tf(EC, L + 8)
        xc = tf(EC, L)
        sk = tf(EC, L)
        dl = tf(EC, L)
        bb = tf(L)
        cc = tf(L)
        dA = tf(2, L)
        uu = tf(2, L)
        hs = tf(2, L)
        sp_e = uu
        dtr = dA
        inT = [tr(EC * P), tr(EC * P)]
        skT = [tr(EC * P), tr(EC * P)]
        spread = tr(NG, P)
        dlh, dll = tr(EC, L), tr(EC, L)
        dxh, dxl = tr(EC, L), tr(EC, L)
        hc = ctx.enter_context(nc.sbuf_tensor("hc", [P, 2, L], F32))

        s2_w = sem("s2_w")
        s2_sel = sem("s2_sel")
        s2_wT = sem("s2_wT")
        s2_wc = sem("s2_wc")
        s2_wl = sem("s2_wl")
        s2_in = sem("s2_in")
        s2_ina = sem("s2_ina")
        s2_conv = sem("s2_conv")
        s2_xc = sem("s2_xc")
        s2_dr = sem("s2_dr")
        s2_drc = sem("s2_drc")
        s2_bc = sem("s2_bc")
        s2_bcc = sem("s2_bcc")
        s2_z = sem("s2_z")
        s2_ab = sem("s2_ab")
        s2_sp = sem("s2_sp")
        s2_dl = sem("s2_dl")
        s2_hi = sem("s2_hi")
        s2_lo = sem("s2_lo")
        s2_pd = sem("s2_pd")
        s2_dA = sem("s2_dA")
        s2_u = sem("s2_u")
        s2_h = sem("s2_h")
        s2_hc = sem("s2_hc")
        s2_yg = sem("s2_yg")
        s2_y = sem("s2_y")
        s2_y2 = sem("s2_y2")
        s2_o = sem("s2_o")

        ORDER = [NG // 4 * j + r for r in range(NG // 4) for j in range(4)]
        N2W = 14

        def s2_load(q, s):
            q.wait_ge(x_done, X_AFTER[s])
            pb = "L0_attn_b_"
            by_channel = [(cb, "conv_b"), (db, "wd2_b"), (wdd, "W_D")]
            q.dma_start(sw_raw, a[pb + "skip_w"].rearrange("(c p) d -> p c d", p=P)).then_inc(s2_w, 16)
            q.dma_start(iw_raw, a[pb + "in_w"].rearrange("(c p) d -> p c d", p=P)).then_inc(s2_w, 16)
            q.dma_start(cw, a[pb + "conv_w"].rearrange("(c p) k -> p c k", p=P)).then_inc(s2_w, 16)
            for t, n in by_channel:
                q.dma_start(t.unsqueeze(2), a[pb + n].rearrange("(c p a) -> p c a", p=P, a=1),
                            allow_slow_non_contiguous=True).then_inc(s2_w, 16)
            q.dma_start(wd1_raw[0:DT], a[pb + "wd1"]).then_inc(s2_w, 16)
            q.dma_start(wd2_raw, a[pb + "wd2"].rearrange("(c p) r -> p c r", p=P)).then_inc(s2_w, 16)
            q.dma_start(wb_raw[0:NS], a[pb + "wb"]).then_inc(s2_w, 16)
            q.dma_start(wc_raw[0:NS], a[pb + "wc"]).then_inc(s2_w, 16)
            q.dma_start(al_raw[0:EC * NG], a[pb + "A_log"].rearrange("(g e) n -> g (e n)", e=EG)).then_inc(s2_w, 16)
            q.dma_start(ow_raw, a[pb + "out_w"]).then_inc(s2_w, 16)
            q.dma_start(gain[:, 0:1], a[pb + "norm_w"].rearrange("(p a) -> p a", a=1)).then_inc(s2_w, 16)
            q.dma_start(gain[:, 1:2], a["L1_attn_a_gamma"].rearrange("a b (p c) -> p (a b c)", c=1)).then_inc(s2_w, 16)
            q.dma_start(gain[:, 2:3], a["L1_attn_a_beta"].rearrange("a b (p c) -> p (a b c)", c=1)).then_inc(s2_w, 16)

        def s2_pool(pool, link, s):
            pool.wait_ge(x_done, X_AFTER[s])
            link(pool.memset(hc[:, :, :], 0.0))
            z = hc[:, :, :].rearrange("p a b -> p (a b)")
            pool.affine_select(out=spread.rearrange("p g (e n) -> p g e n", e=EG),
                               in_=z.rearrange("p (g e n) -> p g e n", g=NG, e=EG),
                               compare_op=ALU.not_equal, fill=1.0, base=0,
                               pattern=[[-EG, NG], [-1, EG], [0, NS]], channel_multiplier=1).then_inc(s2_sel, 1)
            link(pool.memset(gather, 1.0))
            link(pool.affine_select(out=gather, in_=gather, compare_op=ALU.is_ge, fill=0.0, base=0,
                                    pattern=[[EG * NS, 4], [-NS, 32]], channel_multiplier=1))
            link(pool.affine_select(out=gather, in_=gather, compare_op=ALU.is_ge, fill=0.0, base=NS - 1,
                                    pattern=[[-EG * NS, 4], [NS, 32]], channel_multiplier=-1))
            pool.wait_ge(s2_sel, 1)
            pool.memset(xp[:, :, 0:KW - 1], 0.0).then_inc(s2_sel, 1)
            for u in range(B * EC * NG):
                pool.wait_ge(s2_h, u + 1)
                wait(pool, s2_yg, u - 1)
                pool.tensor_tensor(hc[:, u % 2, :], hs[:, u % 2, :], cc, ALU.mult).then_inc(s2_hc, 1)

        def s2_pe(pe, s):
            pe.wait_ge(s2_w, 16 * (N2W + 1))
            for c in range(EC):
                pe.transpose(bank(2)[:, P * c:P * c + P], iw_raw[:, c, :], ident[:, :])
                pe.transpose(bank(2)[:, 256 + P * c:256 + P * c + P], sw_raw[:, c, :], ident[:, :])
            for c in range(EC):
                pe.transpose(bank(3)[:, DT * c:DT * c + DT], wd1_raw[0:DT, P * c:P * c + P], ident[0:DT, 0:DT])
                pe.transpose(bank(3)[0:DT, P + P * c:2 * P + P * c], wd2_raw[:, c, :], ident[:, :])
            pe.transpose(bank(3)[:, 384:384 + EC * NG], al_raw[0:EC * NG, :], ident[0:EC * NG, 0:EC * NG])
            for c in range(EC):
                pe.transpose(bank(4)[:, P * c:P * c + P], ow_raw[:, P * c:P * c + P], ident[:, :])
                pe.transpose(bank(4)[:, 256 + NS * c:256 + NS * c + NS], wb_raw[0:NS, P * c:P * c + P],
                             ident[0:NS, 0:NS])
                ins = pe.transpose(bank(4)[:, 320 + NS * c:320 + NS * c + NS], wc_raw[0:NS, P * c:P * c + P],
                                   ident[0:NS, 0:NS])
            ins.then_inc(s2_wT, 1)
            ln_pe(pe, s)
            pe.wait_ge(s2_wl, 2)
            pe.wait_ge(s2_sel, 2)
            for b in range(B):
                wait(pe, x_done, X_AFTER[s] + b)
                for n in range(8):
                    kind, c, i = n // 4, n // 2 % 2, n % 2
                    pe.wait_ge(ln_lo, 4 * s + 2 * b + i + 1)
                    wait(pe, s2_ina, 8 * b + n - 1)
                    w = (inT, skT)[kind]
                    mm3(pe, bank(6 + n % 2), (w[0][:, P * c:P * c + P], w[1][:, P * c:P * c + P]),
                        xt(L * b + 512 * i, 512)).then_inc(s2_in, 1)
                pe.wait_ge(s2_xc, 2 * b + 2)
                for i in range(2):
                    for c in range(EC):
                        ins = pe.matmul(bank(2 + i)[0:DT, :], wd1T[:, c, :], xc[:, c, 512 * i:512 * i + 512],
                                        start=c == 0, stop=c == EC - 1)
                    ins.then_inc(s2_dr, 1)
                for n in range(4):
                    w, i = (wbT, wcT)[n // 2], n % 2
                    for c in range(EC):
                        ins = pe.matmul(bank(4 + n), w[:, c, :], xc[:, c, 512 * i:512 * i + 512],
                                        start=c == 0, stop=c == EC - 1)
                    ins.then_inc(s2_bc, 1)
                pe.wait_ge(s2_drc, 2 * b + 2)
                for n in range(4):
                    c, i = n // 2, n % 2
                    if n == 0:
                        pe.wait_ge(s2_ina, 8 * b + 8)
                    pe.matmul(bank(n), wd2T[0:DT, P * c:P * c + P], dtr[0:DT, 0, 512 * i:512 * i + 512],
                              start=True, stop=True).then_inc(s2_z, 1)
                pe.wait_ge(s2_bcc, 4 * b + 4)
                pe.wait_ge(s2_sp, 4 * b + 4)

                def bcast(k, c, g):
                    for i in range(2):
                        v = 2 * k + i
                        wait(pe, s2_dA, v - 2)
                        wait(pe, s2_u, v - 2)
                        for j, (hi_, lo_) in enumerate(((dlh, dll), (dxh, dxl))):
                            o = bank(3 * j + v % 3)
                            pe.matmul(o, spread[:, g, :], hi_[:, c, 512 * i:512 * i + 512], start=True, stop=False)
                            ins = pe.matmul(o, spread[:, g, :], lo_[:, c, 512 * i:512 * i + 512], start=False,
                                            stop=True)
                        ins.then_inc(s2_pd, 1)

                def collect(k, n, c, g):
                    pe.wait_ge(s2_hc, k + 1)
                    if n == 0:
                        wait(pe, s2_y2, EC * b + c)
                    j, r = g // 4, g % 4
                    for i in range(2):
                        ins = pe.matmul(bank(6 + i)[32 * j:32 * j + 32, :], gather[:, r, :],
                                        hc[:, k % 2, 512 * i:512 * i + 512], start=r == 0, stop=r == 3)
                    ins.then_inc(s2_yg, 1)

                pe.wait_ge(s2_lo, 4 * b + 4)
                seq = [(c, n, g) for c in range(EC) for n, g in enumerate(ORDER)]
                k0 = b * EC * NG
                bcast(k0, seq[0][0], seq[0][2])
                for k, (c, n, g) in enumerate(seq):
                    if k + 1 < len(seq):
                        bcast(k0 + k + 1, seq[k + 1][0], seq[k + 1][2])
                    if k:
                        pc, pn, pg = seq[k - 1]
                        collect(k0 + k - 1, pn, pc, pg)
                pc, pn, pg = seq[-1]
                collect(k0 + len(seq) - 1, pn, pc, pg)
                pe.wait_ge(s2_y2, EC * (b + 1))
                for t in range(LB):
                    for c in range(EC):
                        ins = pe.matmul(bank(t // 4)[:, P * (t % 4):P * (t % 4) + P], dl[:, c, P * t:P * t + P],
                                        owT[:, c, :], start=c == 0, stop=c == EC - 1)
                ins.then_inc(s2_o, 1)

        def s2_act(act, link, s):
            act.wait_ge(s2_wT, 1)
            act.activation(inT[0], bank(2)[:, 0:256], ACT.Copy).then_inc(s2_wc, 1)
            act.activation(skT[0], bank(2)[:, 256:512], ACT.Copy).then_inc(s2_wc, 1)
            act.activation(wd1T, bank(3)[:, 0:P].rearrange("p (c r) -> p c r", c=EC), ACT.Copy).then_inc(s2_wc, 1)
            act.activation(wd2T[0:DT], bank(3)[0:DT, P:P + E2], ACT.Copy).then_inc(s2_wc, 1)
            link(act.activation(negA, bank(3)[:, 384:384 + EC * NG], ACT.Exp))
            act.activation(negA, negA, ACT.Copy, scale=-1.0).then_inc(s2_wc, 1)
            act.activation(owT, bank(4)[:, 0:256].rearrange("p (c d) -> p c d", c=EC), ACT.Copy).then_inc(s2_wc, 1)
            for w, o in ((wbT, 256), (wcT, 320)):
                for c in range(EC):
                    act.activation(w[:, c, :].rearrange("p (e n) -> p e n", e=EG),
                                   bank(4)[:, o + NS * c:o + NS * c + NS].unsqueeze(1).to_broadcast([P, EG, NS]),
                                   ACT.Copy).then_inc(s2_wc, 1)
            ln_act(act, link, s)
            for b in range(B):
                wait(act, x_done, X_AFTER[s] + b)
                for n in range(8):
                    kind, c, i = n // 4, n // 2 % 2, n % 2
                    act.wait_ge(s2_in, 8 * b + n + 1)
                    if kind == 0:
                        act.activation(xp[:, c, KW - 1 + 512 * i:KW - 1 + 512 * i + 512], bank(6 + n % 2),
                                       ACT.Copy).then_inc(s2_ina, 1)
                    else:
                        act.activation(sk[:, c, 512 * i:512 * i + 512], bank(6 + n % 2), ACT.Silu).then_inc(s2_ina, 1)
                for c in range(EC):
                    act.wait_ge(s2_conv, 2 * b + c + 1)
                    act.activation(xc[:, c, :], uu[:, c, :], ACT.Silu, bias=cb[:, c:c + 1]).then_inc(s2_xc, 1)
                for i in range(2):
                    act.wait_ge(s2_dr, 2 * b + i + 1)
                    act.activation(dtr[0:DT, 0, 512 * i:512 * i + 512], bank(2 + i)[0:DT, :],
                                   ACT.Copy).then_inc(s2_drc, 1)
                for n in range(4):
                    act.wait_ge(s2_bc, 4 * b + n + 1)
                    act.activation((bb, cc)[n // 2][:, 512 * (n % 2):512 * (n % 2) + 512], bank(4 + n),
                                   ACT.Copy).then_inc(s2_bcc, 1)
                act.wait_ge(s2_xc, 2 * b + 2)
                for n in range(4):
                    c, i = n // 2, n % 2
                    act.wait_ge(s2_z, 4 * b + n + 1)
                    act.activation(sp_e[:, c, 512 * i:512 * i + 512], bank(n), ACT.Abs,
                                   bias=db[:, c:c + 1]).then_inc(s2_ab, 1)
                act.wait_ge(s2_ab, 4 * b + 4)
                for c in range(EC):
                    link(act.activation(sp_e[:, c, :], sp_e[:, c, :], ACT.Exp, scale=-1.0))
                for c in range(EC):
                    act.activation(sp_e[:, c, :], sp_e[:, c, :], ACT.Ln, bias=1.0).then_inc(s2_sp, 2)
                for c in range(EC):
                    act.wait_ge(s2_dl, 4 * b + 2 * c + 1)
                    act.activation(dlh[:, c, :], dl[:, c, :], ACT.Copy).then_inc(s2_hi, 1)
                for c in range(EC):
                    act.wait_ge(s2_dl, 4 * b + 2 * c + 2)
                    act.activation(dxh[:, c, :], dA[:, c, :], ACT.Copy).then_inc(s2_hi, 1)
                act.wait_ge(s2_lo, 4 * b + 4)
                for k in range(EC * NG):
                    kk = b * EC * NG + k
                    G = k // NG * NG + ORDER[k % NG]
                    for i in range(2):
                        v = 2 * kk + i
                        act.wait_ge(s2_pd, v + 1)
                        wait(act, s2_h, kk - 1)
                        act.activation(dA[:, kk % 2, 512 * i:512 * i + 512], bank(v % 3), ACT.Exp,
                                       scale=negA[:, G:G + 1]).then_inc(s2_dA, 1)

        def s2_dve(dve, link, s):
            dve.wait_ge(s2_wc, 10)
            dve.tensor_tensor(inT[1], bank(2)[:, 0:256], f32(inT[0]), ALU.subtract).then_inc(s2_wl, 1)
            dve.tensor_tensor(skT[1], bank(2)[:, 256:512], f32(skT[0]), ALU.subtract).then_inc(s2_wl, 1)
            ln_dve(dve, link, s)
            dve.wait_ge(s2_sel, 2)
            for b in range(B):
                for c in range(EC):
                    dve.wait_ge(s2_ina, 8 * b + 2 * c + 2)
                    link(dve.tensor_scalar(uu[:, c, :], xp[:, c, 0:L], cw[:, c, 0:1], None, ALU.mult))
                    for k in range(1, KW):
                        ins = dve.scalar_tensor_tensor(out=uu[:, c, :], in0=xp[:, c, k:k + L],
                                                       scalar=cw[:, c, k:k + 1], in1=uu[:, c, :],
                                                       op0=ALU.mult, op1=ALU.add)
                        if k < KW - 1:
                            link(ins)
                    ins.then_inc(s2_conv, 1)
                for n in range(4):
                    c, i = n // 2, n % 2
                    dve.wait_ge(s2_ab, 4 * b + n + 1)
                    ins = dve.tensor_scalar(dl[:, c, 512 * i:512 * i + 512], bank(n), db[:, c:c + 1], 0.0,
                                            ALU.add, ALU.max)
                    ins.then_inc(chain_dve, 1)
                    link.n += 1
                dve.wait_ge(chain_dve, link.n)
                dve.wait_ge(s2_sp, 4 * b + 4)
                for c in range(EC):
                    dve.tensor_tensor(dl[:, c, :], dl[:, c, :], sp_e[:, c, :], ALU.add).then_inc(s2_dl, 1)
                    dve.wait_ge(s2_dl, 4 * b + 2 * c + 1)
                    dve.tensor_tensor(dA[:, c, :], dl[:, c, :], xc[:, c, :], ALU.mult).then_inc(s2_dl, 1)
                    dve.wait_ge(s2_dl, 4 * b + 2 * c + 2)
                dve.wait_ge(s2_hi, 4 * b + 4)
                for c in range(EC):
                    dve.tensor_tensor(dll[:, c, :], dl[:, c, :], f32(dlh[:, c, :]), ALU.subtract).then_inc(s2_lo, 1)
                    dve.tensor_tensor(dxl[:, c, :], dA[:, c, :], f32(dxh[:, c, :]), ALU.subtract).then_inc(s2_lo, 1)
                dve.wait_ge(s2_lo, 4 * b + 4)
                dve.wait_ge(s2_bcc, 4 * b + 4)

                def gate(c):
                    dve.wait_ge(s2_yg, b * EC * NG + (c + 1) * NG)
                    link(dve.scalar_tensor_tensor(out=dl[:, c, :], in0=xc[:, c, :], scalar=wdd[:, c:c + 1],
                                                  in1=bank(6, 2), op0=ALU.mult, op1=ALU.add))
                    dve.tensor_tensor(dl[:, c, :], dl[:, c, :], sk[:, c, :], ALU.mult).then_inc(s2_y2, 1)

                for k in range(EC * NG):
                    kk = b * EC * NG + k
                    wait(dve, s2_h, kk - 1)
                    for i in range(2):
                        v = 2 * kk + i
                        dve.wait_ge(s2_pd, v + 1)
                        dve.tensor_tensor(uu[:, kk % 2, 512 * i:512 * i + 512], bank(3 + v % 3),
                                          bb[:, 512 * i:512 * i + 512], ALU.mult).then_inc(s2_u, 1)
                    dve.wait_ge(s2_u, 2 * kk + 2)
                    dve.wait_ge(s2_dA, 2 * kk + 2)
                    wait(dve, s2_hc, kk - 1)
                    dve.tensor_tensor_scan(hs[:, kk % 2, :], dA[:, kk % 2, :], uu[:, kk % 2, :], 0.0,
                                           ALU.mult, ALU.add).then_inc(s2_h, 1)
                    if k % NG == 1 and k > NG:
                        gate(k // NG - 1)
                gate(EC - 1)
                dve.wait_ge(s2_o, b + 1)
                xb = X[:, LB * b:LB * b + LB, :].rearrange("p t d -> p (t d)")
                rb_ = R[:, LB * b:LB * b + LB, :].rearrange("p t d -> p (t d)")
                link(dve.tensor_tensor(xb, xb, bank(0, 2), ALU.add))
                dve.tensor_tensor(xb, xb, rb_, ALU.add).then_inc(x_done, 1)
                dve.wait_ge(x_done, X_AFTER[s] + b + 1)

        H4, HD4 = 4, 32
        tf, tr = carver(AF, AF_WORDS), carver(AR, AR_WORDS)
        w4_raw = tf(3 * D)
        wo4_raw = tf(D)
        wq4T = tf(P)
        bout4 = tf(D)
        head_mask = tf(P)
        k4e = tf(L)
        k4t = tf(LB, P)
        v4 = tf(LB, P)
        ctxm = tf(P)
        m2 = tf(P)
        k4m = tf(2)
        k4s = tf(2)
        k4r = tf(2)
        w4h, w4l = tr(3 * D), tr(3 * D)
        g4h, g4l = tr(P), tr(P)

        s4_w = sem("s4_w")
        s4_wt = sem("s4_wt")
        s4_wh = sem("s4_wh")
        s4_wl = sem("s4_wl")
        s4_mask = sem("s4_mask")
        s4_k = sem("s4_k")
        s4_m = sem("s4_m")
        s4_e = sem("s4_e")
        s4_v = sem("s4_v")
        s4_vc = sem("s4_vc")
        s4_kt = sem("s4_kt")
        s4_ktc = sem("s4_ktc")
        s4_c = sem("s4_c")
        s4_cm = sem("s4_cm")
        s4_y = sem("s4_y")

        def s4_load(q, s):
            q.wait_ge(x_done, X_AFTER[s])
            q.dma_start(w4_raw, a["L1_attn_a_w_qkv"]).then_inc(s4_w, 16)
            q.dma_start(wo4_raw, a["L1_attn_a_w_out"]).then_inc(s4_w, 16)
            q.dma_start(bout4[0:1], a["L1_attn_a_b_out"].rearrange("(a d) -> a d", a=1)).then_inc(s4_w, 16)

        def s4_pool(pool, link, s):
            pool.wait_ge(x_done, X_AFTER[s])
            link(pool.memset(head_mask, 0.0))
            for h in range(H4):
                r = HD4 * h
                pool.memset(head_mask[r:r + HD4, r:r + HD4], 1.0).then_inc(s4_mask, 1)

        def s4_pe(pe, s):
            pe.wait_ge(s4_w, 48)
            pe.transpose(bank(2)[:, 0:P], w4_raw[:, 0:D], ident[:, :]).then_inc(s4_wt, 1)
            ln_pe(pe, s)
            pe.wait_ge(s4_wl, 1)
            for b in range(B):
                wait(pe, x_done, X_AFTER[s] + b)
                for i in range(2):
                    pe.wait_ge(ln_lo, 4 * s + 2 * b + i + 1)
                    ins = mm3(pe, bank(4 + i), (w4h[:, D:2 * D], w4l[:, D:2 * D]), xt(L * b + 512 * i, 512))
                ins.then_inc(s4_k, 1)
                for t in range(LB):
                    ins = mm3(pe, bank(6 + t // 4)[:, P * (t % 4):P * (t % 4) + P], xt(L * b + P * t, P),
                              (w4h[:, 2 * D:3 * D], w4l[:, 2 * D:3 * D]))
                ins.then_inc(s4_v, 1)
                pe.wait_ge(s4_e, b + 1)
                for t in range(LB):
                    ins = pe.transpose(bank(4 + t // 4)[:, P * (t % 4):P * (t % 4) + P], k4e[:, P * t:P * t + P],
                                       ident[:, :])
                ins.then_inc(s4_kt, 1)
                pe.wait_ge(s4_vc, b + 1)
                pe.wait_ge(s4_ktc, b + 1)
                for t in range(LB):
                    ins = pe.matmul(bank(2)[:, 0:P], v4[:, t, :], k4t[:, t, :], start=t == 0, stop=t == LB - 1)
                ins.then_inc(s4_c, 1)
                pe.wait_ge(s4_cm, 4 * b + 1)
                pe.matmul(bank(3)[:, 0:P], ctxm, wo4_raw, start=True, stop=True).then_inc(s4_c, 1)
                pe.wait_ge(s4_cm, 4 * b + 2)
                pe.matmul(bank(2)[:, 0:P], wq4T, m2, start=True, stop=True).then_inc(s4_c, 1)
                pe.wait_ge(s4_cm, 4 * b + 4)
                for t in range(LB):
                    o = bank(6 + t // 4)[:, P * (t % 4):P * (t % 4) + P]
                    mm3(pe, o, xt(L * b + P * t, P), (g4h, g4l), stop=False)
                    ins = pe.matmul(o, ones_row[0:1, :], bout4[0:1, :], start=False, stop=True)
                ins.then_inc(s4_y, 1)

        def s4_act(act, link, s):
            act.wait_ge(s4_w, 48)
            act.activation(w4h, w4_raw, ACT.Copy).then_inc(s4_wh, 1)
            act.wait_ge(s4_wt, 1)
            act.activation(wq4T, bank(2)[:, 0:P], ACT.Copy).then_inc(s4_wh, 1)
            ln_act(act, link, s)
            for b in range(B):
                act.wait_ge(s4_m, b + 1)
                act.activation(k4e, bank(4, 2), ACT.Exp, bias=k4m[:, b:b + 1],
                               accum_out=k4s[:, b:b + 1]).then_inc(s4_e, 1)
                act.wait_ge(s4_v, b + 1)
                act.activation(v4.rearrange("p t d -> p (t d)"), bank(6, 2), ACT.Copy).then_inc(s4_vc, 1)
                act.wait_ge(s4_c, 3 * b + 3)
                act.activation(g4h, bank(2)[:, 0:P], ACT.Copy).then_inc(s4_cm, 1)

        def s4_dve(dve, link, s):
            dve.wait_ge(s4_wh, 2)
            dve.tensor_tensor(w4l, w4_raw, f32(w4h), ALU.subtract).then_inc(s4_wl, 1)
            ln_dve(dve, link, s)
            for b in range(B):
                dve.wait_ge(s4_k, b + 1)
                dve.tensor_reduce(k4m[:, b:b + 1], bank(4, 2), AX, ALU.max, negate=True).then_inc(s4_m, 1)
                dve.wait_ge(s4_e, b + 1)
                link(dve.reciprocal(k4r[:, b:b + 1], k4s[:, b:b + 1]))
                dve.wait_ge(s4_kt, b + 1)
                dve.tensor_copy(k4t.rearrange("p t d -> p (t d)"), bank(4, 2)).then_inc(s4_ktc, 1)
                dve.wait_ge(s4_c, 3 * b + 1)
                dve.wait_ge(s4_mask, H4)
                dve.tensor_tensor(ctxm, bank(2)[:, 0:P], head_mask, ALU.mult).then_inc(s4_cm, 1)
                dve.wait_ge(s4_c, 3 * b + 2)
                dve.tensor_scalar(m2, bank(3)[:, 0:P], k4r[:, b:b + 1], HD4 ** -0.5, ALU.mult,
                                  ALU.mult).then_inc(s4_cm, 1)
                dve.wait_ge(s4_cm, 4 * b + 3)
                dve.tensor_tensor(g4l, bank(2)[:, 0:P], f32(g4h), ALU.subtract).then_inc(s4_cm, 1)
                dve.wait_ge(s4_y, b + 1)
                xb = X[:, LB * b:LB * b + LB, :].rearrange("p t d -> p (t d)")
                rb_ = R[:, LB * b:LB * b + LB, :].rearrange("p t d -> p (t d)")
                link(dve.tensor_tensor(xb, xb, bank(6, 2), ALU.add))
                dve.tensor_tensor(xb, xb, rb_, ALU.add).then_inc(x_done, 1)
                dve.wait_ge(x_done, X_AFTER[s] + b + 1)

        H6, HD6 = 16, 8
        HS = 4
        SS = H6 // HS
        QH = 512
        NQ = QH // P
        SUB = 64
        SC6 = HD6 ** -0.5
        POOL_HEADS = 8
        tf, tr = carver(AF, AF_WORDS), carver(AR, AR_WORDS)
        w6_raw = tf(3 * D)
        b6_raw = tf(3 * D)
        wp6 = tf(SS, D)
        bp6 = tf(D)
        b6rep = tf(2 * SS, P)
        bcol = tf(2 * SS, 2)
        lo_q = tf(1)
        lo_k = tf(1)
        sgn_q = tf(1)
        sgn_k = tf(1)
        tmp6 = tf(2, 512)
        mix6 = tf(2, 512)
        v6 = tf(LB, H6 * 32)
        e6 = tf(2, H6 * P)
        p6 = tf(2, H6 * P)
        z6 = tf(2, P)
        w6i = tf(2, P)
        ot6 = tf(2, 512)
        zero6 = tf(HS, P)
        rep_h = tr(2 * SS, P)
        rep_l = tr(2 * SS, P)
        wv_h, wv_l = tr(P), tr(P)
        hi6 = tr(2, 512)
        k6 = tr(SS, L)
        q6 = tr(SS, HS * QH)
        negm6 = ctx.enter_context(nc.sbuf_tensor("negm6", [P, 4, SUB], BF16))

        s6_w = sem("s6_w")
        s6_z = sem("s6_z")
        s6_wp = sem("s6_wp")
        s6_wh = sem("s6_wh")
        s6_wl = sem("s6_wl")
        s6_b = sem("s6_b")
        s6_bc = sem("s6_bc")
        s6_m = sem("s6_m")
        s6_pr = sem("s6_pr")
        s6_tmp = sem("s6_tmp")
        s6_hi = sem("s6_hi")
        s6_st = sem("s6_st")
        s6_v = sem("s6_v")
        s6_vc = sem("s6_vc")
        s6_s = sem("s6_s")
        s6_max = sem("s6_max")
        s6_sub = sem("s6_sub")
        s6_e = sem("s6_e")
        s6_wi = sem("s6_wi")
        s6_pd = sem("s6_pd")
        s6_pp = sem("s6_pp")
        s6_pv = sem("s6_pv")
        s6_ot = sem("s6_ot")
        s6_o = sem("s6_o")

        NPASS = B * (L // QH)
        def projections(b):
            keys = [(1, x, i) for x in range(SS) for i in range(2)]
            return keys

        def s6_load(q, s):
            q.wait_ge(x_done, X_AFTER[s])
            q.dma_start(w6_raw, a["L1_attn_b_w_qkv"]).then_inc(s6_w, 16)
            q.dma_start(b6_raw[0:1], a["L1_attn_b_b_qkv"].rearrange("(a d) -> a d", a=1)).then_inc(s6_w, 16)
            q.dma_start(bp6[0:1], a["L1_attn_b_b_proj"].rearrange("(a d) -> a d", a=1)).then_inc(s6_w, 16)
            q.wait_ge(s6_z, 2)
            for i in range(HS):
                q.dma_start(wp6[32 * i:32 * i + HD6, :, :],
                            a["L1_attn_b_w_proj"].rearrange("(x i d) c -> i d x c", x=SS, i=HS)[i]).then_inc(s6_wp, 16)

        TILES = [(qt, kb) for qt in range(NQ) for kb in range(LB)]
        NTI = len(TILES)

        def proj_list(p):
            b, half = p // 2, p % 2
            keys = [(1, x, i) for x in range(SS) for i in range(2)] if half == 0 else []
            return keys + [(0, x, half) for x in range(SS)]

        PROJ_AT = [sum(len(proj_list(k)) for k in range(p)) for p in range(NPASS + 1)]

        def s6_pool(pool, link, s):
            pool.wait_ge(x_done, X_AFTER[s])
            pool.memset(wp6, 0.0).then_inc(s6_z, 1)
            pool.memset(q6.rearrange("p a b -> p (a b)").bitcast(F32), 0.0).then_inc(s6_z, 1)
            pool.memset(v6, 0.0).then_inc(s6_z, 1)
            for p in range(NPASS):
                for t, (qt, kb) in enumerate(TILES):
                    m = NTI * p + t
                    pool.wait_ge(s6_wi, m + 1)
                    wait(pool, s6_pv, m - 1)
                    n = POOL_HEADS
                    pool.tensor_tensor(p6[:, m % 2, 0:n * P].rearrange("p (h q) -> p h q", h=n),
                                       e6[:, m % 2, 0:n * P].rearrange("p (h q) -> p h q", h=n),
                                       w6i[:, m % 2, :].unsqueeze(1).to_broadcast([P, n, P]),
                                       ALU.mult).then_inc(s6_pp, 1)

        def s6_pe(pe, s):
            pe.wait_ge(s6_bc, 1)
            for x in range(2 * SS):
                ins = pe.matmul(bank(2)[:, 2 * x:2 * x + 2], b6rep[0:1, x, :], ones_row[0:1, 0:2], start=True,
                                stop=True)
            ins.then_inc(s6_b, 1)
            ln_pe(pe, s)
            pe.wait_ge(s6_wl, 2)
            pe.wait_ge(s6_z, 3)
            pe.wait_ge(s6_wp, 16 * HS)
            pe.wait_ge(ln_lo, 4 * s + 4)
            pe.wait_ge(s6_bc, 2)
            for p in range(NPASS):
                b, half = p // 2, p % 2
                if p:
                    pe.wait_ge(s6_e, 2 * NTI * p)
                for n, (kind, x, i) in enumerate(proj_list(p)):
                    m = PROJ_AT[p] + n
                    wait(pe, s6_tmp, m - 1)
                    w = SS * kind + x
                    mm3(pe, bank(m % 2), (rep_h[:, w, :], rep_l[:, w, :]),
                        xt(L * b + 512 * i, 512)).then_inc(s6_pr, 1)
                if half == 0:
                    for t in range(LB):
                        o = bank(2 + t // 4)[:, P * (t % 4):P * (t % 4) + P]
                        mm3(pe, o, xt(L * b + P * t, P), (wv_h, wv_l), stop=False)
                        ins = pe.matmul(o, ones_row[0:1, :], b6_raw[0:1, 2 * D:3 * D], start=False, stop=True)
                    ins.then_inc(s6_v, 1)
                pe.wait_ge(s6_st, PROJ_AT[p + 1])
                pe.wait_ge(s6_vc, b + 1)

                def scores(j):
                    qt, kb = TILES[j // 2]
                    m = 2 * NTI * p + j
                    wait(pe, s6_e, m - 2)
                    for x in range(SS):
                        q = q6[:, x, :].rearrange("p (i q) -> p i q", i=HS)
                        q0 = P * qt + SUB * (j % 2)
                        ins = pe.matmul(bank(2 * (m % 3) + x // 2)[:, 256 * (x % 2):256 * (x % 2) + 256],
                                        k6[:, x, P * kb:P * kb + P], q[:, :, q0:q0 + SUB],
                                        start=x % 2 == 0, stop=True, skip_group_check=True)
                    ins.then_inc(s6_s, 1)

                def subtract(j):
                    m = 2 * NTI * p + j
                    pe.wait_ge(s6_max, m + 1)
                    for h in range(2):
                        ins = pe.matmul(bank(2 * (m % 3) + h).rearrange("p (h q) -> p h q", h=8), ident_bf[:, :],
                                        negm6[:, m % 4, :].unsqueeze(1).to_broadcast([P, 8, SUB]), start=False,
                                        stop=True, skip_group_check=True)
                    ins.then_inc(s6_sub, 1)

                def pv(t):
                    qt, kb = TILES[t]
                    m = NTI * p + t
                    pe.wait_ge(s6_pp, m + 1)
                    pe.wait_ge(s6_pd, m + 1)
                    if kb == 0:
                        wait(pe, x_done, X_AFTER[s] + m // LB - 1)
                    for x in range(SS):
                        for i in range(HS):
                            h = HS * x + i
                            ins = pe.matmul(bank(6 + m // LB % 2)[32 * i:32 * i + 32, P * x:P * x + P],
                                            v6[:, kb, 32 * h:32 * h + 32], p6[:, m % 2, P * h:P * h + P],
                                            start=kb == 0 and x == 0, stop=kb == LB - 1, skip_group_check=True)
                    ins.then_inc(s6_pv, 1)

                def project(g):
                    pe.wait_ge(s6_ot, g + 1)
                    o = bank(6 + g % 2)[:, 0:P]
                    for x in range(SS):
                        pe.matmul(o, ot6[:, g % 2, P * x:P * x + P], wp6[:, x, :], start=x == 0, stop=False)
                    pe.matmul(o, ones_row[0:1, :], bp6[0:1, :], start=False, stop=True).then_inc(s6_o, 1)

                scores(0)
                scores(1)
                for j in range(2 * NTI):
                    subtract(j)
                    if j + 2 < 2 * NTI:
                        scores(j + 2)
                    t = j // 2 - 2
                    if j % 2 and t >= 0:
                        pv(t)
                        if t % LB == LB - 1:
                            project(NQ * p + t // LB)
                pv(NTI - 2)
                pv(NTI - 1)
                project(NQ * p + NQ - 1)

        def s6_act(act, link, s):
            act.wait_ge(s6_w, 48)
            for kind in range(2):
                src = w6_raw[:, D * kind:D * kind + D].rearrange("p (x i d) -> p x i d", x=SS, i=HS)
                bsrc = b6_raw[0:1, D * kind:D * kind + D].rearrange("p (x i d) -> p x i d", x=SS, i=HS)
                for x in range(SS):
                    w = SS * kind + x
                    act.activation(rep_h[:, w, :].rearrange("p (i c d) -> p i c d", i=HS, c=4),
                                   src[:, x].unsqueeze(2).to_broadcast([P, HS, 4, HD6]),
                                   ACT.Copy).then_inc(chain_act, 1)
                    act.activation(b6rep[0:1, w, :].rearrange("p (i c d) -> p i c d", i=HS, c=4),
                                   bsrc[:, x].unsqueeze(2).to_broadcast([1, HS, 4, HD6]),
                                   ACT.Copy).then_inc(chain_act, 1)
                    link.n += 2
            link(act.activation(wv_h, w6_raw[:, 2 * D:3 * D], ACT.Copy))
            act.sem_inc(s6_wh, 1)
            act.sem_inc(s6_bc, 1)
            ln_act(act, link, s)
            act.wait_ge(s6_b, 1)
            act.activation(bcol[:, 0:SS, :], bank(2)[:, 0:2 * SS].rearrange("p (x a) -> p x a", a=2), ACT.Copy,
                           scale=SC6).then_inc(chain_act, 1)
            link.n += 1
            link(act.activation(bcol[:, SS:, :], bank(2)[:, 2 * SS:4 * SS].rearrange("p (x a) -> p x a", a=2),
                                ACT.Copy))
            act.sem_inc(s6_bc, 1)
            for p in range(NPASS):
                b, half = p // 2, p % 2
                for n, (kind, x, i) in enumerate(proj_list(p)):
                    m = PROJ_AT[p] + n
                    act.wait_ge(s6_pr, m + 1)
                    wait(act, s6_st, m - 1)
                    act.activation(tmp6[:, m % 2, :], bank(m % 2), ACT.Identity,
                                   bias=bcol[:, SS * kind + x, 0:1],
                                   scale=SC6 if kind == 0 else 1.0).then_inc(s6_tmp, 1)
                    act.wait_ge(s6_tmp, m + 1)
                    act.activation(hi6[:, m % 2, :], tmp6[:, m % 2, :], ACT.Copy).then_inc(s6_hi, 1)
                if half == 0:
                    act.wait_ge(s6_v, b + 1)
                    for i in range(2):
                        ins = act.activation(
                            v6[:, 4 * i:4 * i + 4, :].rearrange("p t (h c) -> p t h c", h=H6)[:, :, :, 0:HD6],
                            bank(2 + i).rearrange("p (t h d) -> p t h d", t=4, h=H6), ACT.Copy)
                        if i == 0:
                            link(ins)
                    ins.then_inc(s6_vc, 1)
                for j in range(2 * NTI):
                    m = 2 * NTI * p + j
                    act.wait_ge(s6_sub, m + 1)
                    if j % 2 == 0:
                        wait(act, s6_pp, m // 2 - 1)
                        wait(act, s6_pd, m // 2 - 1)
                    o = e6[:, m // 2 % 2, :].rearrange("p (h q) -> p h q", h=H6)
                    q0 = SUB * (j % 2)
                    act.activation(o[:, :, q0:q0 + SUB], bank(2 * (m % 3), 2).rearrange("p (h q) -> p h q", h=H6),
                                   ACT.Exp).then_inc(s6_e, 1)
                    t = j // 2 - 2
                    if j % 2 and t >= 0 and t % LB == LB - 1:
                        flush(act, NQ * p + t // LB)
                flush(act, NQ * p + NQ - 1)

        def flush(act, g):
            act.wait_ge(s6_pv, LB * (g + 1))
            wait(act, s6_o, g - 1)
            act.activation(ot6[:, g % 2, :], bank(6 + g % 2), ACT.Copy).then_inc(s6_ot, 1)

        def s6_dve(dve, link, s):
            dve.wait_ge(s6_wh, 1)
            for kind in range(2):
                src = w6_raw[:, D * kind:D * kind + D].rearrange("p (x i d) -> p x i d", x=SS, i=HS)
                for x in range(SS):
                    w = SS * kind + x
                    ins = dve.tensor_tensor(rep_l[:, w, :].rearrange("p (i c d) -> p i c d", i=HS, c=4),
                                            src[:, x].unsqueeze(2).to_broadcast([P, HS, 4, HD6]),
                                            f32(rep_h[:, w, :]).rearrange("p (i c d) -> p i c d", i=HS, c=4),
                                            ALU.subtract)
                    if w < 2 * SS - 1:
                        ins.then_inc(chain_dve, 1)
                        link.n += 1
            ins.then_inc(s6_wl, 1)
            dve.tensor_tensor(wv_l, w6_raw[:, 2 * D:3 * D], f32(wv_h), ALU.subtract).then_inc(s6_wl, 1)
            idq = ident[:, :].rearrange("p (i r) -> p i r", i=HS)[:, :, 16:32]
            idk = ident[:, :].rearrange("p (i r) -> p i r", i=2 * HS)[:, :, 8:16]
            link(dve.tensor_reduce(lo_q, idq, mybir.AxisListType.XY, ALU.add))
            link(dve.tensor_reduce(lo_k, idk, mybir.AxisListType.XY, ALU.add))
            link(dve.tensor_scalar(sgn_q, lo_q, -2.0, 1.0, ALU.mult, ALU.add))
            link(dve.tensor_scalar(sgn_k, lo_k, -2.0, 1.0, ALU.mult, ALU.add))
            ln_dve(dve, link, s)
            dve.wait_ge(s6_z, 2)
            for p in range(NPASS):
                b, half = p // 2, p % 2
                if p:
                    dve.wait_ge(s6_s, 2 * NTI * p)
                for n, (kind, x, i) in enumerate(proj_list(p)):
                    m = PROJ_AT[p] + n
                    lo, sgn = (lo_q, sgn_q) if kind == 0 else (lo_k, sgn_k)
                    dve.wait_ge(s6_hi, m + 1)
                    link(dve.tensor_scalar(mix6[:, m % 2, :], f32(hi6[:, m % 2, :]), sgn, None, ALU.mult))
                    if kind == 1:
                        dve.scalar_tensor_tensor(out=k6[:, x, 512 * i:512 * i + 512], in0=tmp6[:, m % 2, :],
                                                 scalar=lo, in1=mix6[:, m % 2, :], op0=ALU.mult,
                                                 op1=ALU.add).then_inc(s6_st, 1)
                    else:
                        for j in range(HS):
                            r = slice(32 * j, 32 * j + 32)
                            ins = dve.scalar_tensor_tensor(out=q6[r, x, QH * j:QH * j + QH], in0=tmp6[r, m % 2, :],
                                                           scalar=lo[r], in1=mix6[r, m % 2, :], op0=ALU.mult,
                                                           op1=ALU.add)
                            if j < HS - 1:
                                ins.then_inc(chain_dve, 1)
                                link.n += 1
                        ins.then_inc(s6_st, 1)

                def maxima(j):
                    m = 2 * NTI * p + j
                    dve.wait_ge(s6_s, m + 1)
                    wait(dve, s6_sub, m - 3)
                    dve.tensor_reduce(negm6[:, m % 4, :],
                                      bank(2 * (m % 3), 2).rearrange("p (h q) -> p q h", h=H6), AX, ALU.max,
                                      negate=True).then_inc(s6_max, 1)

                def normalise(t):
                    m = NTI * p + t
                    dve.wait_ge(s6_e, 2 * m + 2)
                    e = e6[:, m % 2, :].rearrange("p (h q) -> p h q", h=H6)
                    link(dve.tensor_reduce(z6[:, m % 2, :], e6[:, m % 2, :].rearrange("p (h q) -> p q h", h=H6), AX,
                                           ALU.add))
                    wait(dve, s6_pp, m - 1)
                    dve.reciprocal(w6i[:, m % 2, :], z6[:, m % 2, :]).then_inc(s6_wi, 1)
                    dve.wait_ge(s6_wi, m + 1)
                    wait(dve, s6_pv, m - 1)
                    n = H6 - POOL_HEADS
                    dve.tensor_tensor(p6[:, m % 2, POOL_HEADS * P:].rearrange("p (h q) -> p h q", h=n),
                                      e[:, POOL_HEADS:, :], w6i[:, m % 2, :].unsqueeze(1).to_broadcast([P, n, P]),
                                      ALU.mult).then_inc(s6_pd, 1)

                def add(g):
                    dve.wait_ge(s6_o, g + 1)
                    dve.tensor_tensor(X[:, g, :], X[:, g, :], bank(6 + g % 2)[:, 0:P], ALU.add).then_inc(x_done, 1)

                for j in range(2 * NTI):
                    maxima(j)
                    if j % 2 == 0 and j >= 2:
                        normalise(j // 2 - 1)
                    t = j // 2 - 3
                    if j % 2 and t >= 0 and t % LB == LB - 1:
                        add(NQ * p + t // LB)
                normalise(NTI - 1)
                add(NQ * p + NQ - 1)
            dve.wait_ge(x_done, X_AFTER[s + 1])

        PE = {0: s0_pe, 1: s1_pe, 2: s2_pe, 3: s1_pe, 4: s4_pe, 5: moe_pe, 6: s6_pe, 7: moe_pe}
        ACTS = {0: s0_act, 1: s1_act, 2: s2_act, 3: s1_act, 4: s4_act, 5: moe_act, 6: s6_act, 7: moe_act}
        DVE = {0: s0_dve, 1: s1_dve, 2: s2_dve, 3: s1_dve, 4: s4_dve, 5: moe_dve, 6: s6_dve, 7: moe_dve}
        POOL = {2: s2_pool, 4: s4_pool, 6: s6_pool}
        LOAD = {1: s1_load, 2: s2_load, 3: s1_load, 4: s4_load, 5: moe_load, 6: s6_load, 7: moe_load}
        X_AFTER = {1: 2, 2: 6, 3: 8, 4: 12, 5: 14, 6: 18, 7: 34, 8: 38}

        block = ctx.enter_context(nc.Block())

        @block.sync
        def _(sp):
            sp.dma_start(X[:, :, :], x_dram).then_inc(x_loaded, 16)
            s0_load(sp)
            for s in range(1, upto):
                LOAD[s](sp, s)
            sp.wait_ge(x_done, X_AFTER[upto])
            sp.dma_start(out_dram, X[:, :, :]).then_inc(out_sem, 16)
            sp.wait_ge(out_sem, 16)

        @block.gpsimd
        def _(pool):
            link = Chain(pool, chain_pool)
            link(pool.memset(ident[:, :], 0.0))
            link(pool.affine_select(out=ident[:, :], in_=ident[:, :], compare_op=ALU.not_equal, fill=1.0,
                                    base=0, pattern=[[-1, P]], channel_multiplier=1))
            link(pool.tensor_copy(ident_bf[:, :], ident[:, :]))
            link(pool.memset(causal_bf[:, :], 0.0))
            link(pool.affine_select(out=causal_bf[:, :], in_=causal_bf[:, :], compare_op=ALU.is_ge, fill=MASKED,
                                    base=0, pattern=[[-1, P]], channel_multiplier=1))
            link(pool.memset(half_pow[:, :], -0.5))
            pool.memset(ones_row[:, :], 1.0).then_inc(consts_ready, 1)
            for s in range(upto):
                ln_pool(pool, link, s)
                if s in POOL:
                    POOL[s](pool, link, s)

        @block.tensor
        def _(pe):
            for s in range(upto):
                PE[s](pe) if s == 0 else PE[s](pe, s)

        @block.scalar
        def _(act):
            link = Chain(act, chain_act)
            for s in range(upto):
                ACTS[s](act, link) if s == 0 else ACTS[s](act, link, s)

        @block.vector
        def _(dve):
            link = Chain(dve, chain_dve)
            for s in range(upto):
                DVE[s](dve, link) if s == 0 else DVE[s](dve, link, s)


_INS = ['L0_attn_a_x_bld', 'L0_attn_a_Wq', 'L0_attn_a_Wkv_down', 'L0_attn_a_Wk_up', 'L0_attn_a_Wv_up',
        'L0_attn_a_Wout', 'L0_attn_b_norm_w', 'L0_attn_b_skip_w', 'L0_attn_b_in_w', 'L0_attn_b_conv_w',
        'L0_attn_b_conv_b', 'L0_attn_b_wd1', 'L0_attn_b_wd2', 'L0_attn_b_wd2_b', 'L0_attn_b_wb', 'L0_attn_b_wc',
        'L0_attn_b_A_log', 'L0_attn_b_W_D', 'L0_attn_b_out_w', 'L0_ffn_W_fc', 'L0_ffn_W_proj',
        'L1_attn_a_gamma', 'L1_attn_a_beta', 'L1_attn_a_w_qkv', 'L1_attn_a_w_out', 'L1_attn_a_b_out',
        'L1_attn_b_w_qkv', 'L1_attn_b_b_qkv', 'L1_attn_b_w_proj', 'L1_attn_b_b_proj',
        'L1_ffn_Wg', 'L1_ffn_Wu', 'L1_ffn_Wd']


def kernel(**inputs):
    import numpy as np
    import concourse.bacc as bacc
    from concourse.bass_utils import run_bass_kernel_spmd as run

    nc = bacc.Bacc("TRN2", target_bir_lowering=False, num_devices=1)
    arrays, a = {}, {}
    for name in _INS:
        v = np.ascontiguousarray(inputs[name])
        arrays[f"in_{name}_dram"] = v
        a[name] = nc.dram_tensor(f"in_{name}_dram", v.shape, mybir.dt.from_np(v.dtype), kind="ExternalInput").ap()
    out = nc.dram_tensor("out_dram", (B, L, D), F32, kind="ExternalOutput").ap()
    build(nc, a, out)
    r = run(nc, [arrays], core_ids=[0])
    return r.results[0]["out_dram"]
```

```python
from contextlib import ExitStack

import numpy as np

import concourse.bass as bass
from concourse import mybir

ALU = mybir.AluOpType
ACT = mybir.ActivationFunctionType
AX = mybir.AxisListType.X
F32 = mybir.dt.float32
F32R = mybir.dt.float32r
BF16 = mybir.dt.bfloat16

P = 128
B, L, D = 2, 1024, 128
T = B * L
NB = T // P
LB = L // P
EPS = 1e-5
MASKED = -3.0e38
AF_WORDS, AR_WORDS = 21 * 1024, 17664


def wait(eng, sem, n):
    if n > 0:
        eng.wait_ge(sem, n)


class Chain:

    def __init__(self, eng, sem):
        self.eng, self.sem, self.n = eng, sem, 0

    def __call__(self, ins):
        self.n += 1
        ins.then_inc(self.sem, 1)
        self.eng.wait_ge(self.sem, self.n)


def mm3(pe, out, lhs, rhs, start=True, stop=True):
    (ah, al), (bh, bl) = lhs, rhs
    pe.matmul(out, ah, bh, start=start, stop=False)
    pe.matmul(out, ah, bl, start=False, stop=False)
    return pe.matmul(out, al, bh, start=False, stop=stop)


def f32(ap):
    return ap.bitcast(F32)


def build(nc, a, out, upto=8):
    ctx = ExitStack()
    with ctx:
        def sb(name, shape, dt=F32):
            return ctx.enter_context(nc.sbuf_tensor(name, shape, dt))

        def sem(name):
            return ctx.enter_context(nc.semaphore(name))

        ps = ctx.enter_context(nc.psum_tensor("ps", [P, 8, 512], F32))

        def bank(i, n=1):
            return ps[:, i:i + n, :].rearrange("p b c -> p (b c)")

        ident = sb("ident", [P, P])
        ident_bf = sb("ident_bf", [P, P], BF16)
        causal_bf = sb("causal_bf", [P, P], BF16)
        half_pow = sb("half_pow", [P, NB])
        ones_row = sb("ones_row", [1, P])
        X = sb("X", [P, NB, D])
        R = sb("R", [P, NB, D])
        XN = sb("XN", [P, NB, D])
        XH = sb("XH", [P, T], F32R)
        XL = sb("XL", [P, T], F32R)
        stats = sb("stats", [P, NB, 6])
        mv = sb("mv", [P, NB, 2])
        var_eps = sb("var_eps", [P, NB])
        rstd = sb("rstd", [P, NB])
        gain = sb("gain", [P, 3])
        lnt = sb("lnt", [P, 2, 512])
        AF = sb("AF", [P, AF_WORDS])
        AR = sb("AR", [P, AR_WORDS], F32R)

        def carver(arena, total):
            at = [0]

            def take(*shape):
                n = 1
                for s in shape:
                    n *= s
                lo = at[0]
                at[0] += n
                assert at[0] <= total, (at[0], total)
                v = arena[:, lo:lo + n]
                if len(shape) == 2:
                    v = v.rearrange("p (a b) -> p a b", a=shape[0])
                if len(shape) == 3:
                    v = v.rearrange("p (a b c) -> p a b c", a=shape[0], b=shape[1])
                return v
            return take

        chain_dve = sem("chain_dve")
        chain_act = sem("chain_act")
        chain_pool = sem("chain_pool")
        consts_ready = sem("consts_ready")
        x_loaded = sem("x_loaded")
        ln_stat = sem("ln_stat")
        ln_rstd = sem("ln_rstd")
        ln_norm = sem("ln_norm")
        ln_tr = sem("ln_tr")
        ln_hi = sem("ln_hi")
        ln_lo = sem("ln_lo")
        x_done = sem("x_done")
        out_sem = sem("out_sem")

        x_dram = a["L0_attn_a_x_bld"].rearrange("b (n p) d -> p (b n) d", p=P)
        out_dram = out.rearrange("b (n p) d -> p (b n) d", p=P)

        DOUBLE = (2, 4)

        def rounds(s):
            return s + sum(1 for k in DOUBLE if k < s)

        def ln_dve(dve, link, s, per_batch=None):
            def stat(src, r):
                for t in range(NB):
                    dve.bn_stats(stats[:, t, :], src[:, t, :]).then_inc(chain_dve, 1)
                    link.n += 1
                dve.wait_ge(chain_dve, link.n)
                for t in range(NB):
                    ins = dve.bn_aggr(mv[:, t, :], stats[:, t, :])
                    ins.then_inc(ln_stat, 1)
                dve.wait_ge(ln_stat, NB * (r + 1))
                dve.wait_ge(ln_rstd, r + 1)
            r = rounds(s)
            if s == 0:
                dve.wait_ge(x_loaded, 16)
            stat(X, r)
            for t in range(NB):
                dve.tensor_scalar(R[:, t, :], X[:, t, :], mv[:, t, 0:1], rstd[:, t:t + 1],
                                  ALU.subtract, ALU.mult).then_inc(ln_norm if s not in DOUBLE else chain_dve, 1)
                if s in DOUBLE:
                    link.n += 1
            if s in DOUBLE:
                dve.wait_ge(chain_dve, link.n)
                stat(R, r + 1)
                for t in range(NB):
                    if s == 4:
                        ins = dve.tensor_scalar(XN[:, t, :], R[:, t, :], mv[:, t, 0:1], rstd[:, t:t + 1],
                                                ALU.subtract, ALU.mult)
                    else:
                        ins = dve.tensor_scalar(XN[:, t, :], R[:, t, :], rstd[:, t:t + 1], None, ALU.mult)
                    ins.then_inc(ln_norm, 1)
            for i in range(4):
                dve.wait_ge(ln_hi, 4 * s + i + 1)
                src = lnt[:, i % 2, :] if s in DOUBLE else bank(i % 2)
                dve.tensor_tensor(XL[:, 512 * i:512 * i + 512], src, f32(XH[:, 512 * i:512 * i + 512]),
                                  ALU.subtract).then_inc(ln_lo, 1)

        def ln_pool(pool, link, s):
            for k in range(2 if s in DOUBLE else 1):
                r = rounds(s) + k
                pool.wait_ge(ln_stat, NB * (r + 1))
                if s == 2 and k == 1:
                    link(pool.tensor_tensor(var_eps[:, :], mv[:, :, 0], mv[:, :, 0], ALU.mult))
                    link(pool.tensor_tensor(var_eps[:, :], var_eps[:, :], mv[:, :, 1], ALU.add))
                    link(pool.tensor_scalar(var_eps[:, :], var_eps[:, :], EPS, None, ALU.add))
                else:
                    link(pool.tensor_scalar(var_eps[:, :], mv[:, :, 1], EPS, None, ALU.add))
                pool.tensor_tensor(rstd[:, :], var_eps[:, :], half_pow[:, :], ALU.pow).then_inc(ln_rstd, 1)

        def ln_pe(pe, s):
            src = XN if s in DOUBLE else R
            for i in range(4):
                pe.wait_ge(ln_norm, NB * s + 4 * i + 4)
                if i >= 2:
                    pe.wait_ge(ln_lo, 4 * s + i - 1)
                for j in range(4):
                    ins = pe.transpose(bank(i % 2)[:, P * j:P * j + P], src[:, 4 * i + j, :], ident[:, :])
                ins.then_inc(ln_tr, 1)

        def ln_act(act, link, s):
            for i in range(4):
                act.wait_ge(ln_tr, 4 * s + i + 1)
                hi = XH[:, 512 * i:512 * i + 512]
                if s in DOUBLE:
                    if i >= 2:
                        act.wait_ge(ln_lo, 4 * s + i - 1)
                    g = gain[:, 0:1] if s == 2 else gain[:, 1:2]
                    b = 0.0 if s == 2 else gain[:, 2:3]
                    link(act.activation(lnt[:, i % 2, :], bank(i % 2), ACT.Identity, scale=g, bias=b))
                    act.activation(hi, lnt[:, i % 2, :], ACT.Copy).then_inc(ln_hi, 1)
                else:
                    act.activation(hi, bank(i % 2), ACT.Copy).then_inc(ln_hi, 1)

        def xt(lo, n):
            return XH[:, lo:lo + n], XL[:, lo:lo + n]

        H0, HD, LD = 16, 64, 32
        G0 = H0 // 4
        tf, tr = carver(AF, AF_WORDS), carver(AR, AR_WORDS)
        wq_raw = tf(H0 * HD)
        wkup_raw = tf(H0 * HD)
        wvup_raw = tf(H0 * HD)
        wout_raw = tf(8, D)
        wkv_raw = tf(LD)
        wqT = tf(H0 * HD)
        wkT = tf(8, LD)
        wvT = tf(8, LD)
        a32 = tf(H0, LD)
        bcomb = tf(G0, D)
        lat_tok = tf(LB, LD)
        rinv_x = tf(LB, P)
        rb = tf(L)
        ot = tf(G0, L)
        pm = tf(2, L)
        pt = tf(4, 512)
        negm = tf(4)
        rsum = tf(4)
        rinv = tf(LB, 4)
        arep = [tr(H0, P), tr(H0, P)]
        wkv4 = [tr(P), tr(P)]
        kst = tr(L)
        qst = tr(4, L)

        s0_w = sem("s0_w")
        s0_wT = sem("s0_wT")
        s0_wTc = sem("s0_wTc")
        s0_ab = sem("s0_ab")
        s0_ahi = sem("s0_ahi")
        s0_alo = sem("s0_alo")
        s0_lat = sem("s0_lat")
        s0_khi = sem("s0_khi")
        s0_klo = sem("s0_klo")
        s0_latc = sem("s0_latc")
        s0_q = sem("s0_q")
        s0_qhi = sem("s0_qhi")
        s0_qlo = sem("s0_qlo")
        s0_s = sem("s0_s")
        s0_m = sem("s0_m")
        s0_e = sem("s0_e")
        s0_ri = sem("s0_ri")
        s0_t = sem("s0_t")
        s0_ca = sem("s0_ca")
        s0_cd = sem("s0_cd")
        s0_pv = sem("s0_pv")
        s0_rx = sem("s0_rx")
        s0_rp = sem("s0_rp")
        s0_rc = sem("s0_rc")
        s0_ot = sem("s0_ot")
        s0_y = sem("s0_y")

        STEPS = [(hh, qb) for hh in range(4) for qb in range(LB)]
        CH = [(u, c, min(4, qb + 1 - 4 * c)) for u, (hh, qb) in enumerate(STEPS) for c in range((qb + 4) // 4)]
        FIRST_CH = [next(i for i, x in enumerate(CH) if x[0] == u) for u in range(len(STEPS))] + [len(CH)]
        NU, NC = len(STEPS), len(CH)

        def on_dve(i):
            return i % 3 == 0

        def copies(i, dve):
            full, rest = divmod(i, NC)
            per = sum(1 for k in range(NC) if on_dve(k) == dve)
            return full * per + sum(1 for k in range(rest) if on_dve(k) == dve)

        def copied(eng, n):
            wait(eng, s0_cd, copies(n, True))
            wait(eng, s0_ca, copies(n, False))

        def s0_load(q):
            q.dma_start(wq_raw, a["L0_attn_a_Wq"].rearrange("d h k -> d (h k)")).then_inc(s0_w, 16)
            q.dma_start(wkup_raw[0:LD], a["L0_attn_a_Wk_up"].rearrange("d h k -> d (h k)")).then_inc(s0_w, 16)
            q.dma_start(wvup_raw[0:LD], a["L0_attn_a_Wv_up"].rearrange("d h k -> d (h k)")).then_inc(s0_w, 16)
            q.dma_start(wout_raw, a["L0_attn_a_Wout"].rearrange("(j h) k o -> (h k) j o", h=2)).then_inc(s0_w, 16)
            q.dma_start(wkv_raw, a["L0_attn_a_Wkv_down"]).then_inc(s0_w, 16)

        def s0_pe(pe):
            pe.wait_ge(s0_w, 80)
            pe.wait_ge(consts_ready, 1)
            for j in range(8):
                pe.transpose(bank(2 + j // 4)[:, P * (j % 4):P * (j % 4) + P], wq_raw[:, P * j:P * j + P], ident[:, :])
                pe.transpose(bank(4)[:, LD * j:LD * j + LD], wkup_raw[0:LD, P * j:P * j + P], ident[0:LD, 0:LD])
                ins = pe.transpose(bank(4)[:, 256 + LD * j:256 + LD * j + LD], wvup_raw[0:LD, P * j:P * j + P],
                                   ident[0:LD, 0:LD])
            ins.then_inc(s0_wT, 1)
            pe.wait_ge(s0_wTc, 3)
            for h in range(H0):
                r, j = 64 * (h % 2), h // 2
                pe.matmul(bank(5 + 2 * (h % 2))[:, LD * j:LD * j + LD], wqT[r:r + 64, P * j:P * j + P], wkT[r:r + 64, j, :],
                          start=True, stop=True)
            for h in range(H0):
                r, j, c = 64 * (h % 2), h // 2, LD * (h % 4)
                ins = pe.matmul(bank(6 if h % 2 == 0 else 2)[c:c + LD, P * (h // 4):P * (h // 4) + P], wvT[r:r + 64, j, :],
                                wout_raw[r:r + 64, j, :], start=True, stop=True)
            ins.then_inc(s0_ab, 1)
            ln_pe(pe, 0)
            pe.wait_ge(s0_alo, 2)
            for b in range(B):
                if b:
                    pe.wait_ge(x_done, b)
                for i in range(2):
                    pe.wait_ge(ln_lo, 2 * b + i + 1)
                    mm3(pe, bank(2 + i), (wkv4[0], wkv4[1]), xt(L * b + 512 * i, 512)).then_inc(s0_lat, 1)
                for t in range(LB):
                    ins = mm3(pe, bank(4)[:, LD * t:LD * t + LD], xt(L * b + P * t, P),
                              (wkv4[0][:, 0:LD], wkv4[1][:, 0:LD]))
                ins.then_inc(s0_lat, 1)
                pe.wait_ge(s0_klo, 2 * b + 2)
                pe.wait_ge(s0_latc, b + 1)
                for g in range(G0):
                    gg = b * G0 + g
                    wait(pe, s0_ot, gg)
                    for n in range(8):
                        hh, i = n // 2, n % 2
                        if n >= 4:
                            pe.wait_ge(s0_qlo, 8 * gg + n - 3)
                        mm3(pe, bank(n % 4), (arep[0][:, 4 * g + hh, :], arep[1][:, 4 * g + hh, :]),
                            xt(L * b + 512 * i, 512)).then_inc(s0_q, 1)
                    pe.wait_ge(s0_qlo, 8 * gg + 8)

                    def scores(u):
                        hh, qb = STEPS[u]
                        if u >= 2:
                            pe.wait_ge(s0_e, NU * gg + u - 1)
                        for c in range((qb + 4) // 4):
                            n = min(4, qb + 1 - 4 * c) * P
                            o = bank(2 * (u % 2) + c)
                            pe.matmul(o[:, 0:n], qst[:, hh, P * qb:P * qb + P], kst[:, 512 * c:512 * c + n],
                                      start=True, stop=True)
                        pe.matmul(o[:, n - P:n], ident_bf[:, :], causal_bf[:, :], start=False, stop=True,
                                  skip_group_check=True).then_inc(s0_s, 1)

                    def turn(u):
                        pe.wait_ge(s0_e, NU * gg + u + 1)
                        for i in range(FIRST_CH[u], FIRST_CH[u + 1]):
                            _, c, n = CH[i]
                            k = NC * gg + i
                            copied(pe, k - 1)
                            for j in range(n):
                                ins = pe.transpose(bank(4 + k % 2)[:, P * j:P * j + P],
                                                   pm[:, u % 2, P * (4 * c + j):P * (4 * c + j) + P], ident[:, :])
                            ins.then_inc(s0_t, 1)

                    def pv(u):
                        hh, qb = STEPS[u]
                        for i in range(FIRST_CH[u], FIRST_CH[u + 1]):
                            _, c, n = CH[i]
                            k = NC * gg + i
                            copied(pe, k + 1)
                            for j in range(n):
                                kb = 4 * c + j
                                ins = pe.matmul(bank(6 + qb // 4)[LD * hh:LD * hh + LD, P * (qb % 4):P * (qb % 4) + P],
                                                lat_tok[:, kb, :], pt[:, k % 4, P * j:P * j + P],
                                                start=kb == 0, stop=kb == qb)
                            ins.then_inc(s0_pv, 1)

                    scores(0)
                    for u in range(NU):
                        if u + 1 < NU:
                            scores(u + 1)
                        turn(u)
                        if u:
                            pv(u - 1)
                    pv(NU - 1)
                    pe.wait_ge(s0_rx, gg + 1)
                    for qb in range(LB):
                        ins = pe.matmul(bank(qb // 4)[:, P * (qb % 4):P * (qb % 4) + P], rinv_x[:, qb, :],
                                        ident[:, :], start=True, stop=True)
                    ins.then_inc(s0_rp, 1)
                pe.wait_ge(s0_ot, G0 * (b + 1))
                for t in range(LB):
                    for g in range(G0):
                        ins = pe.matmul(bank(2 + t // 4)[:, P * (t % 4):P * (t % 4) + P], ot[:, g, P * t:P * t + P],
                                        bcomb[:, g, :], start=g == 0, stop=g == G0 - 1)
                ins.then_inc(s0_y, 1)

        def s0_act(act, link):
            act.wait_ge(s0_wT, 1)
            act.activation(wqT, bank(2, 2), ACT.Copy).then_inc(s0_wTc, 1)
            act.activation(wkT, bank(4)[:, 0:256].rearrange("p (j c) -> p j c", j=8), ACT.Copy).then_inc(s0_wTc, 1)
            act.activation(wvT, bank(4)[:, 256:512].rearrange("p (j c) -> p j c", j=8), ACT.Copy).then_inc(s0_wTc, 1)
            act.wait_ge(s0_ab, 1)
            for r in range(2):
                act.activation(a32.rearrange("p (j r) c -> p j r c", r=2)[:, :, r, :],
                               bank(5 + 2 * r)[:, 0:256].rearrange("p (j c) -> p j c", j=8), ACT.Copy,
                               scale=HD ** -0.5).then_inc(chain_act, 1)
                link.n += 1
            for h in range(4):
                c = LD * h
                act.activation(bcomb[c:c + LD], bank(6 if h % 2 == 0 else 2)[c:c + LD].rearrange(
                    "p (g o) -> p g o", g=G0), ACT.Copy).then_inc(chain_act, 1)
                link.n += 1
            act.wait_ge(chain_act, link.n)
            act.activation(arep[0].rearrange("p h (r c) -> p h r c", r=4),
                           a32.unsqueeze(2).to_broadcast([P, H0, 4, LD]), ACT.Copy).then_inc(s0_ahi, 1)
            act.activation(wkv4[0].rearrange("p (r c) -> p r c", r=4),
                           wkv_raw.unsqueeze(1).to_broadcast([P, 4, LD]), ACT.Copy).then_inc(s0_ahi, 1)
            ln_act(act, link, 0)
            for b in range(B):
                for i in range(2):
                    act.wait_ge(s0_lat, 3 * b + i + 1)
                    act.activation(kst[:, 512 * i:512 * i + 512], bank(2 + i), ACT.Copy).then_inc(s0_khi, 1)
                act.wait_ge(s0_lat, 3 * b + 3)
                act.activation(lat_tok, bank(4)[:, 0:LB * LD].rearrange("p (t c) -> p t c", t=LB),
                               ACT.Copy).then_inc(s0_latc, 1)
                for g in range(G0):
                    gg = b * G0 + g
                    for n in range(8):
                        act.wait_ge(s0_q, 8 * gg + n + 1)
                        act.activation(qst[:, n // 2, 512 * (n % 2):512 * (n % 2) + 512], bank(n % 4),
                                       ACT.Copy).then_inc(s0_qhi, 1)

                    def copy_chunks(u):
                        for i in range(FIRST_CH[u], FIRST_CH[u + 1]):
                            if on_dve(i):
                                continue
                            k, n = NC * gg + i, CH[i][2] * P
                            act.wait_ge(s0_t, k + 1)
                            wait(act, s0_pv, k - 3)
                            act.activation(pt[:, k % 4, 0:n], bank(4 + k % 2)[:, 0:n], ACT.Copy).then_inc(s0_ca, 1)

                    for u, (hh, qb) in enumerate(STEPS):
                        n = (qb + 1) * P
                        act.wait_ge(s0_m, NU * gg + u + 1)
                        if u >= 2:
                            act.wait_ge(s0_t, NC * gg + FIRST_CH[u - 1])
                        if NU * gg + u >= 4:
                            act.wait_ge(s0_ri, NU * gg + u - 3)
                        act.activation(pm[:, u % 2, 0:n], bank(2 * (u % 2), 2)[:, 0:n], ACT.Exp,
                                       bias=negm[:, u % 4:u % 4 + 1],
                                       accum_out=rsum[:, u % 4:u % 4 + 1]).then_inc(s0_e, 1)
                        if u:
                            copy_chunks(u - 1)
                    copy_chunks(NU - 1)
                    act.wait_ge(s0_ri, NU * gg + NU)
                    act.activation(rinv_x.rearrange("p t (h c) -> p t h c", h=4),
                                   rinv.unsqueeze(3).to_broadcast([P, LB, 4, LD]), ACT.Copy).then_inc(s0_rx, 1)
                    act.wait_ge(s0_rp, gg + 1)
                    act.activation(rb, bank(0, 2), ACT.Copy).then_inc(s0_rc, 1)

        def s0_dve(dve, link):
            dve.wait_ge(s0_ahi, 2)
            dve.tensor_tensor(arep[1].rearrange("p h (r c) -> p h r c", r=4),
                              a32.unsqueeze(2).to_broadcast([P, H0, 4, LD]),
                              f32(arep[0]).rearrange("p h (r c) -> p h r c", r=4), ALU.subtract).then_inc(s0_alo, 1)
            dve.tensor_tensor(wkv4[1].rearrange("p (r c) -> p r c", r=4),
                              wkv_raw.unsqueeze(1).to_broadcast([P, 4, LD]),
                              f32(wkv4[0]).rearrange("p (r c) -> p r c", r=4), ALU.subtract).then_inc(s0_alo, 1)
            ln_dve(dve, link, 0)
            for b in range(B):
                for i in range(2):
                    dve.wait_ge(s0_khi, 2 * b + i + 1)
                    for r in (32, 96):
                        k = kst[r:r + 32, 512 * i:512 * i + 512]
                        ins = dve.tensor_tensor(k, bank(2 + i)[r:r + 32], f32(k), ALU.subtract)
                    ins.then_inc(s0_klo, 1)
                for g in range(G0):
                    gg = b * G0 + g
                    for n in range(8):
                        dve.wait_ge(s0_qhi, 8 * gg + n + 1)
                        q = qst[64:128, n // 2, 512 * (n % 2):512 * (n % 2) + 512]
                        dve.tensor_tensor(q, bank(n % 4)[64:128], f32(q), ALU.subtract).then_inc(s0_qlo, 1)

                    def finish(u):
                        hh, qb = STEPS[u]
                        dve.wait_ge(s0_e, NU * gg + u + 1)
                        dve.reciprocal(rinv[:, qb, hh:hh + 1], rsum[:, u % 4:u % 4 + 1]).then_inc(s0_ri, 1)
                        for i in range(FIRST_CH[u], FIRST_CH[u + 1]):
                            if not on_dve(i):
                                continue
                            k, n = NC * gg + i, CH[i][2] * P
                            dve.wait_ge(s0_t, k + 1)
                            wait(dve, s0_pv, k - 3)
                            dve.tensor_copy(pt[:, k % 4, 0:n], bank(4 + k % 2)[:, 0:n]).then_inc(s0_cd, 1)

                    if gg:
                        dve.wait_ge(s0_rx, gg)
                    for u, (hh, qb) in enumerate(STEPS):
                        n = (qb + 1) * P
                        dve.wait_ge(s0_s, NU * gg + u + 1)
                        if u >= 4 or gg:
                            dve.wait_ge(s0_e, NU * gg + u - 3)
                        dve.tensor_reduce(negm[:, u % 4:u % 4 + 1], bank(2 * (u % 2), 2)[:, 0:n], AX, ALU.max,
                                          negate=True).then_inc(s0_m, 1)
                        if u:
                            finish(u - 1)
                    finish(NU - 1)
                    dve.wait_ge(s0_rc, gg + 1)
                    dve.wait_ge(s0_pv, NC * (gg + 1))
                    wait(dve, s0_y, b)
                    dve.tensor_tensor(ot[:, g, :], bank(6, 2), rb, ALU.mult).then_inc(s0_ot, 1)
                dve.wait_ge(s0_y, b + 1)
                xb = X[:, LB * b:LB * b + LB, :].rearrange("p t d -> p (t d)")
                ins = dve.tensor_tensor(xb, xb, bank(2, 2), ALU.add).then_inc(x_done, 1)
                dve.wait_ge(x_done, b + 1)

        FF = 4
        tf, tr = carver(AF, AF_WORDS), carver(AR, AR_WORDS)
        wfc_raw = tf(FF, D)
        wpj_raw = tf(FF * P)
        wpjT = tf(FF, D)
        ffr = tf(2, 512)
        ffh = tf(2, FF, 512)
        cnt = tf(2, 512)
        yv = tf(2, 512)
        fcT = [tr(FF * P), tr(FF * P)]

        def spike_thresholds(steps=5, beta=0.9, threshold=1.0):
            f = np.float32

            def spikes(y):
                mem, n = f(0), 0
                for _ in range(steps):
                    reset = f(1) if mem - f(threshold) > 0 else f(0)
                    mem = f(f(f(beta) * mem) + y) - reset * f(threshold)
                    n += int(mem - f(threshold) > 0)
                return n
            found = []
            for k in range(1, steps + 1):
                lo, hi = f(0), f(4)
                while np.nextafter(lo, hi) < hi:
                    mid = f((lo + hi) / f(2))
                    lo, hi = (lo, mid) if spikes(mid) >= k else (mid, hi)
                found.append(float(lo))
            return found

        THR = spike_thresholds()

        s1_w = sem("s1_w")
        s1_wT = sem("s1_wT")
        s1_fhi = sem("s1_fhi")
        s1_flo = sem("s1_flo")
        s1_z = sem("s1_z")
        s1_r = sem("s1_r")
        s1_h = sem("s1_h")
        s1_y = sem("s1_y")
        s1_yc = sem("s1_yc")

        def s1_load(q, s):
            q.wait_ge(x_done, X_AFTER[s])
            q.dma_start(wfc_raw, a["L0_ffn_W_fc"].rearrange("(c p) d -> p c d", p=P)).then_inc(s1_w, 16)
            q.dma_start(wpj_raw, a["L0_ffn_W_proj"]).then_inc(s1_w, 16)

        def s1_pe(pe, s):
            k = s // 2
            pe.wait_ge(s1_w, 32 * (k + 1))
            for c in range(FF):
                pe.transpose(bank(2)[:, P * c:P * c + P], wfc_raw[:, c, :], ident[:, :])
            for c in range(FF):
                ins = pe.transpose(bank(3)[:, P * c:P * c + P], wpj_raw[:, P * c:P * c + P], ident[:, :])
            ins.then_inc(s1_wT, 1)
            ln_pe(pe, s)
            pe.wait_ge(s1_flo, k + 1)
            for i in range(4):
                pe.wait_ge(ln_lo, 4 * s + i + 1)
                for c in range(FF):
                    n = 16 * k + 4 * i + c
                    wait(pe, s1_h, n - 1)
                    mm3(pe, bank(2 + n % 2), (fcT[0][:, P * c:P * c + P], fcT[1][:, P * c:P * c + P]),
                        xt(512 * i, 512)).then_inc(s1_z, 1)
                if i:
                    down(pe, k, i - 1)
            down(pe, k, 3)

        def down(pe, k, i):
            n = 4 * k + i
            pe.wait_ge(s1_h, 16 * k + 4 * i + 4)
            wait(pe, s1_yc, n - 1)
            for t in range(4):
                for c in range(FF):
                    ins = pe.matmul(bank(4 + n % 2)[:, P * t:P * t + P], ffh[:, i % 2, c, P * t:P * t + P],
                                    wpjT[:, c, :], start=c == 0, stop=c == FF - 1)
            ins.then_inc(s1_y, 1)

        def s1_act(act, link, s):
            k = s // 2
            act.wait_ge(s1_wT, k + 1)
            act.activation(fcT[0], bank(2), ACT.Copy).then_inc(s1_fhi, 1)
            link(act.activation(wpjT, bank(3).rearrange("p (c d) -> p c d", c=FF), ACT.Copy))
            ln_act(act, link, s)
            for n in range(16 * k, 16 * k + 16):
                act.wait_ge(s1_z, n + 1)
                wait(act, s1_h, n - 1)
                act.activation(ffr[:, n % 2, :], bank(2 + n % 2), ACT.Relu).then_inc(s1_r, 1)

        def s1_dve(dve, link, s):
            k = s // 2
            dve.wait_ge(s1_fhi, k + 1)
            dve.tensor_tensor(fcT[1], bank(2), f32(fcT[0]), ALU.subtract).then_inc(s1_flo, 1)
            ln_dve(dve, link, s)

            def spikes(i):
                n = 4 * k + i
                dve.wait_ge(s1_y, n + 1)
                y, c = yv[:, i % 2, :], cnt[:, i % 2, :]
                dve.tensor_copy(y, bank(4 + n % 2)).then_inc(s1_yc, 1)
                dve.wait_ge(s1_yc, n + 1)
                link(dve.tensor_scalar(c, y, THR[0], None, ALU.is_gt))
                for thr in THR[1:]:
                    link(dve.scalar_tensor_tensor(out=c, in0=y, scalar=thr, in1=c, op0=ALU.is_gt, op1=ALU.add))
                xs = X[:, 4 * i:4 * i + 4, :].rearrange("p t d -> p (t d)")
                dve.scalar_tensor_tensor(out=xs, in0=c, scalar=1.0 / len(THR), in1=xs, op0=ALU.mult,
                                         op1=ALU.add).then_inc(x_done, 1)

            for i in range(4):
                for c in range(FF):
                    n = 16 * k + 4 * i + c
                    dve.wait_ge(s1_r, n + 1)
                    if i >= 2:
                        dve.wait_ge(s1_y, 4 * k + i - 1)
                    dve.scalar_tensor_tensor(out=ffh[:, i % 2, c, :], in0=bank(2 + n % 2), scalar=0.0,
                                             in1=ffr[:, n % 2, :], op0=ALU.max, op1=ALU.mult).then_inc(s1_h, 1)
                if i:
                    spikes(i - 1)
            spikes(3)
            dve.wait_ge(x_done, X_AFTER[s + 1])

        NE, FE = 8, 4
        tf, tr = carver(AF, AF_WORDS), carver(AR, AR_WORDS)
        WCOL = 3 * FE * P
        mraw = tf(2, WCOL)
        msg = tf(3, 512)
        mh = tf(3, 512)
        macc = tf(4, 512)
        mwh = [tr(WCOL), tr(WCOL)]
        mwl = [tr(WCOL), tr(WCOL)]
        mhh = tr(3, 512)
        mhl = tr(3, 512)

        m_w = sem("m_w")
        m_w2 = sem("m_w2")
        m_wh = sem("m_wh")
        m_wl = sem("m_wl")
        m_gu = sem("m_gu")
        m_sg = sem("m_sg")
        m_h = sem("m_h")
        m_hh = sem("m_hh")
        m_hl = sem("m_hl")
        m_d = sem("m_d")
        m_y = sem("m_y")
        m_acc = sem("m_acc")
        m_tr = sem("m_tr")

        NT = 4
        PER = NE * NT * FE

        def moe_load(q, s):
            k = (s - 5) // 2
            q.wait_ge(x_done, X_AFTER[s])
            for e in range(NE):
                n = NE * k + e
                wait(q, m_wl, n - 1)
                w = mraw[:, n % 2, :]
                r = (m_w, m_w2)[n % 2]
                q.dma_start(w[:, 0:512], a["L1_ffn_Wg"][e]).then_inc(r, 16)
                q.dma_start(w[:, 512:1024], a["L1_ffn_Wu"][e]).then_inc(r, 16)
                q.dma_start(w[:, 1024:WCOL].rearrange("p (c d) -> p c d", c=FE),
                            a["L1_ffn_Wd"][e].rearrange("(c p) d -> p c d", p=P)).then_inc(r, 16)

        def moe_weights(n):
            return mwh[n % 2], mwl[n % 2]

        def moe_pe(pe, s):
            k = (s - 5) // 2
            ln_pe(pe, s)

            def up(n):
                e, i, c = n // (NT * FE), n // FE % NT, n % FE
                m = PER * k + n
                if n % (NT * FE) == 0:
                    pe.wait_ge(m_wl, NE * k + e + 1)
                pe.wait_ge(ln_lo, 4 * s + i + 1)
                wait(pe, m_h, m - 2)
                wh, wl = moe_weights(NE * k + e)
                for g in range(2):
                    o = 512 * g + P * c
                    ins = mm3(pe, bank(3 * g + m % 3), (wh[:, o:o + P], wl[:, o:o + P]), xt(512 * i, 512))
                ins.then_inc(m_gu, 1)

            def down_e(n):
                e, i, c = n // (NT * FE), n // FE % NT, n % FE
                m = PER * k + n
                pe.wait_ge(m_hl, m + 1)
                wh, wl = moe_weights(NE * k + e)
                o = 1024 + P * c
                if c == 0:
                    wait(pe, m_acc, m // FE - 1)
                mm3(pe, bank(6 + m // FE % 2), (wh[:, o:o + P], wl[:, o:o + P]),
                    (mhh[:, m % 3, :], mhl[:, m % 3, :]), start=c == 0, stop=c == FE - 1).then_inc(m_d, 1)

            pe.wait_ge(ln_lo, 4 * s + 4)
            up(0)
            up(1)
            for n in range(PER):
                if n + 2 < PER:
                    up(n + 2)
                down_e(n)
            for i in range(NT):
                pe.wait_ge(m_acc, NE * NT * (k + 1) - NT + i + 1)
                for t in range(4):
                    ins = pe.transpose(bank(i % 2)[:, P * t:P * t + P], macc[:, i, P * t:P * t + P], ident[:, :])
                ins.then_inc(m_tr, 1)
                if i == 1:
                    pe.wait_ge(x_done, X_AFTER[s] + 2)

        def moe_act(act, link, s):
            k = (s - 5) // 2

            def split(n):
                act.wait_ge((m_w, m_w2)[n % 2], 48 * (n // 2 + 1))
                wait(act, m_d, NT * FE * (n - 1))
                act.activation(mwh[n % 2], mraw[:, n % 2, :], ACT.Copy).then_inc(m_wh, 1)

            split(NE * k)
            ln_act(act, link, s)
            for n in range(PER):
                m = PER * k + n
                act.wait_ge(m_gu, m + 1)
                wait(act, m_h, m - 2)
                act.activation(msg[:, m % 3, :], bank(m % 3), ACT.Silu).then_inc(m_sg, 1)
                if n:
                    hi(act, m - 1)
                if n % (NT * FE) == 2 and n // (NT * FE) + 1 < NE:
                    split(NE * k + n // (NT * FE) + 1)
            hi(act, PER * k + PER - 1)

        def hi(act, m):
            act.wait_ge(m_h, m + 1)
            wait(act, m_d, m - 2)
            act.activation(mhh[:, m % 3, :], mh[:, m % 3, :], ACT.Copy).then_inc(m_hh, 1)

        def moe_dve(dve, link, s):
            k = (s - 5) // 2

            def split(n):
                dve.wait_ge(m_wh, n + 1)
                dve.tensor_tensor(mwl[n % 2], mraw[:, n % 2, :], f32(mwh[n % 2]), ALU.subtract).then_inc(m_wl, 1)

            def finish(n):
                m = PER * k + n
                dve.wait_ge(m_hh, m + 1)
                dve.tensor_tensor(mhl[:, m % 3, :], mh[:, m % 3, :], f32(mhh[:, m % 3, :]),
                                  ALU.subtract).then_inc(m_hl, 1)

            def total(q):
                e, i = q // NT, q % NT
                dve.wait_ge(m_d, FE * (NE * NT * k + q + 1))
                o = bank(6 + q % 2)
                if e == 0:
                    dve.tensor_copy(macc[:, i, :], o).then_inc(m_acc, 1)
                else:
                    dve.tensor_tensor(macc[:, i, :], macc[:, i, :], o, ALU.add).then_inc(m_acc, 1)

            split(NE * k)
            ln_dve(dve, link, s)
            for n in range(PER):
                m = PER * k + n
                dve.wait_ge(m_sg, m + 1)
                wait(dve, m_hl, m - 2)
                dve.tensor_tensor(mh[:, m % 3, :], bank(3 + m % 3), msg[:, m % 3, :], ALU.mult).then_inc(m_h, 1)
                if n:
                    finish(n - 1)
                if n % FE == 2 and n > FE:
                    total(n // FE - 1)
                if n % (NT * FE) == 3 and n // (NT * FE) + 1 < NE:
                    split(NE * k + n // (NT * FE) + 1)
            finish(PER - 1)
            total(NE * NT - 1)
            for i in range(NT):
                dve.wait_ge(m_tr, NT * k + i + 1)
                xs = X[:, 4 * i:4 * i + 4, :].rearrange("p t d -> p (t d)")
                dve.tensor_tensor(xs, xs, bank(i % 2), ALU.add).then_inc(x_done, 1)
            dve.wait_ge(x_done, X_AFTER[s + 1])

        E2, NS, DT, KW = 256, 16, 64, 4
        EC = E2 // P
        EG = P // NS
        NG = P // EG
        tf, tr = carver(AF, AF_WORDS), carver(AR, AR_WORDS)
        sw_raw = tf(EC, D)
        iw_raw = tf(EC, D)
        cw = tf(EC, KW)
        cb = tf(EC)
        db = tf(EC)
        wdd = tf(EC)
        wd1_raw = tf(E2)
        wd2_raw = tf(EC, DT)
        wb_raw = tf(E2)
        wc_raw = tf(E2)
        al_raw = tf(P)
        ow_raw = tf(E2)
        wd1T = tf(EC, DT)
        wd2T = tf(E2)
        wbT = tf(EC, P)
        wcT = tf(EC, P)
        negA = tf(EC * NG)
        owT = tf(EC, D)
        gather = tf(4, 32)
        xp = tf(EC, L + 8)
        xc = tf(EC, L)
        sk = tf(EC, L)
        dl = tf(EC, L)
        bb = tf(L)
        cc = tf(L)
        dA = tf(2, L)
        uu = tf(2, L)
        hs = tf(2, L)
        sp_e = uu
        dtr = dA
        inT = [tr(EC * P), tr(EC * P)]
        skT = [tr(EC * P), tr(EC * P)]
        spread = tr(NG, P)
        dlh, dll = tr(EC, L), tr(EC, L)
        dxh, dxl = tr(EC, L), tr(EC, L)
        hc = ctx.enter_context(nc.sbuf_tensor("hc", [P, 2, L], F32))

        s2_w = sem("s2_w")
        s2_sel = sem("s2_sel")
        s2_wT = sem("s2_wT")
        s2_wc = sem("s2_wc")
        s2_wl = sem("s2_wl")
        s2_in = sem("s2_in")
        s2_ina = sem("s2_ina")
        s2_conv = sem("s2_conv")
        s2_xc = sem("s2_xc")
        s2_dr = sem("s2_dr")
        s2_drc = sem("s2_drc")
        s2_bc = sem("s2_bc")
        s2_bcc = sem("s2_bcc")
        s2_z = sem("s2_z")
        s2_ab = sem("s2_ab")
        s2_sp = sem("s2_sp")
        s2_dl = sem("s2_dl")
        s2_hi = sem("s2_hi")
        s2_lo = sem("s2_lo")
        s2_pd = sem("s2_pd")
        s2_dA = sem("s2_dA")
        s2_u = sem("s2_u")
        s2_h = sem("s2_h")
        s2_hc = sem("s2_hc")
        s2_yg = sem("s2_yg")
        s2_y = sem("s2_y")
        s2_y2 = sem("s2_y2")
        s2_o = sem("s2_o")

        ORDER = [NG // 4 * j + r for r in range(NG // 4) for j in range(4)]
        N2W = 14

        def s2_load(q, s):
            q.wait_ge(x_done, X_AFTER[s])
            pb = "L0_attn_b_"
            by_channel = [(cb, "conv_b"), (db, "wd2_b"), (wdd, "W_D")]
            q.dma_start(sw_raw, a[pb + "skip_w"].rearrange("(c p) d -> p c d", p=P)).then_inc(s2_w, 16)
            q.dma_start(iw_raw, a[pb + "in_w"].rearrange("(c p) d -> p c d", p=P)).then_inc(s2_w, 16)
            q.dma_start(cw, a[pb + "conv_w"].rearrange("(c p) k -> p c k", p=P)).then_inc(s2_w, 16)
            for t, n in by_channel:
                q.dma_start(t.unsqueeze(2), a[pb + n].rearrange("(c p a) -> p c a", p=P, a=1),
                            allow_slow_non_contiguous=True).then_inc(s2_w, 16)
            q.dma_start(wd1_raw[0:DT], a[pb + "wd1"]).then_inc(s2_w, 16)
            q.dma_start(wd2_raw, a[pb + "wd2"].rearrange("(c p) r -> p c r", p=P)).then_inc(s2_w, 16)
            q.dma_start(wb_raw[0:NS], a[pb + "wb"]).then_inc(s2_w, 16)
            q.dma_start(wc_raw[0:NS], a[pb + "wc"]).then_inc(s2_w, 16)
            q.dma_start(al_raw[0:EC * NG], a[pb + "A_log"].rearrange("(g e) n -> g (e n)", e=EG)).then_inc(s2_w, 16)
            q.dma_start(ow_raw, a[pb + "out_w"]).then_inc(s2_w, 16)
            q.dma_start(gain[:, 0:1], a[pb + "norm_w"].rearrange("(p a) -> p a", a=1)).then_inc(s2_w, 16)
            q.dma_start(gain[:, 1:2], a["L1_attn_a_gamma"].rearrange("a b (p c) -> p (a b c)", c=1)).then_inc(s2_w, 16)
            q.dma_start(gain[:, 2:3], a["L1_attn_a_beta"].rearrange("a b (p c) -> p (a b c)", c=1)).then_inc(s2_w, 16)

        def s2_pool(pool, link, s):
            pool.wait_ge(x_done, X_AFTER[s])
            link(pool.memset(hc[:, :, :], 0.0))
            z = hc[:, :, :].rearrange("p a b -> p (a b)")
            pool.affine_select(out=spread.rearrange("p g (e n) -> p g e n", e=EG),
                               in_=z.rearrange("p (g e n) -> p g e n", g=NG, e=EG),
                               compare_op=ALU.not_equal, fill=1.0, base=0,
                               pattern=[[-EG, NG], [-1, EG], [0, NS]], channel_multiplier=1).then_inc(s2_sel, 1)
            link(pool.memset(gather, 1.0))
            link(pool.affine_select(out=gather, in_=gather, compare_op=ALU.is_ge, fill=0.0, base=0,
                                    pattern=[[EG * NS, 4], [-NS, 32]], channel_multiplier=1))
            link(pool.affine_select(out=gather, in_=gather, compare_op=ALU.is_ge, fill=0.0, base=NS - 1,
                                    pattern=[[-EG * NS, 4], [NS, 32]], channel_multiplier=-1))
            pool.wait_ge(s2_sel, 1)
            pool.memset(xp[:, :, 0:KW - 1], 0.0).then_inc(s2_sel, 1)
            for u in range(B * EC * NG):
                pool.wait_ge(s2_h, u + 1)
                wait(pool, s2_yg, u - 1)
                pool.tensor_tensor(hc[:, u % 2, :], hs[:, u % 2, :], cc, ALU.mult).then_inc(s2_hc, 1)

        def s2_pe(pe, s):
            pe.wait_ge(s2_w, 16 * (N2W + 1))
            for c in range(EC):
                pe.transpose(bank(2)[:, P * c:P * c + P], iw_raw[:, c, :], ident[:, :])
                pe.transpose(bank(2)[:, 256 + P * c:256 + P * c + P], sw_raw[:, c, :], ident[:, :])
            for c in range(EC):
                pe.transpose(bank(3)[:, DT * c:DT * c + DT], wd1_raw[0:DT, P * c:P * c + P], ident[0:DT, 0:DT])
                pe.transpose(bank(3)[0:DT, P + P * c:2 * P + P * c], wd2_raw[:, c, :], ident[:, :])
            pe.transpose(bank(3)[:, 384:384 + EC * NG], al_raw[0:EC * NG, :], ident[0:EC * NG, 0:EC * NG])
            for c in range(EC):
                pe.transpose(bank(4)[:, P * c:P * c + P], ow_raw[:, P * c:P * c + P], ident[:, :])
                pe.transpose(bank(4)[:, 256 + NS * c:256 + NS * c + NS], wb_raw[0:NS, P * c:P * c + P],
                             ident[0:NS, 0:NS])
                ins = pe.transpose(bank(4)[:, 320 + NS * c:320 + NS * c + NS], wc_raw[0:NS, P * c:P * c + P],
                                   ident[0:NS, 0:NS])
            ins.then_inc(s2_wT, 1)
            ln_pe(pe, s)
            pe.wait_ge(s2_wl, 2)
            pe.wait_ge(s2_sel, 2)
            for b in range(B):
                wait(pe, x_done, X_AFTER[s] + b)
                for n in range(8):
                    kind, c, i = n // 4, n // 2 % 2, n % 2
                    pe.wait_ge(ln_lo, 4 * s + 2 * b + i + 1)
                    wait(pe, s2_ina, 8 * b + n - 1)
                    w = (inT, skT)[kind]
                    mm3(pe, bank(6 + n % 2), (w[0][:, P * c:P * c + P], w[1][:, P * c:P * c + P]),
                        xt(L * b + 512 * i, 512)).then_inc(s2_in, 1)
                pe.wait_ge(s2_xc, 2 * b + 2)
                for i in range(2):
                    for c in range(EC):
                        ins = pe.matmul(bank(2 + i)[0:DT, :], wd1T[:, c, :], xc[:, c, 512 * i:512 * i + 512],
                                        start=c == 0, stop=c == EC - 1)
                    ins.then_inc(s2_dr, 1)
                for n in range(4):
                    w, i = (wbT, wcT)[n // 2], n % 2
                    for c in range(EC):
                        ins = pe.matmul(bank(4 + n), w[:, c, :], xc[:, c, 512 * i:512 * i + 512],
                                        start=c == 0, stop=c == EC - 1)
                    ins.then_inc(s2_bc, 1)
                pe.wait_ge(s2_drc, 2 * b + 2)
                for n in range(4):
                    c, i = n // 2, n % 2
                    if n == 0:
                        pe.wait_ge(s2_ina, 8 * b + 8)
                    pe.matmul(bank(n), wd2T[0:DT, P * c:P * c + P], dtr[0:DT, 0, 512 * i:512 * i + 512],
                              start=True, stop=True).then_inc(s2_z, 1)
                pe.wait_ge(s2_bcc, 4 * b + 4)
                pe.wait_ge(s2_sp, 4 * b + 4)

                def bcast(k, c, g):
                    for i in range(2):
                        v = 2 * k + i
                        wait(pe, s2_dA, v - 2)
                        wait(pe, s2_u, v - 2)
                        for j, (hi_, lo_) in enumerate(((dlh, dll), (dxh, dxl))):
                            o = bank(3 * j + v % 3)
                            pe.matmul(o, spread[:, g, :], hi_[:, c, 512 * i:512 * i + 512], start=True, stop=False)
                            ins = pe.matmul(o, spread[:, g, :], lo_[:, c, 512 * i:512 * i + 512], start=False,
                                            stop=True)
                        ins.then_inc(s2_pd, 1)

                def collect(k, n, c, g):
                    pe.wait_ge(s2_hc, k + 1)
                    if n == 0:
                        wait(pe, s2_y2, EC * b + c)
                    j, r = g // 4, g % 4
                    for i in range(2):
                        ins = pe.matmul(bank(6 + i)[32 * j:32 * j + 32, :], gather[:, r, :],
                                        hc[:, k % 2, 512 * i:512 * i + 512], start=r == 0, stop=r == 3)
                    ins.then_inc(s2_yg, 1)

                pe.wait_ge(s2_lo, 4 * b + 4)
                seq = [(c, n, g) for c in range(EC) for n, g in enumerate(ORDER)]
                k0 = b * EC * NG
                bcast(k0, seq[0][0], seq[0][2])
                for k, (c, n, g) in enumerate(seq):
                    if k + 1 < len(seq):
                        bcast(k0 + k + 1, seq[k + 1][0], seq[k + 1][2])
                    if k:
                        pc, pn, pg = seq[k - 1]
                        collect(k0 + k - 1, pn, pc, pg)
                pc, pn, pg = seq[-1]
                collect(k0 + len(seq) - 1, pn, pc, pg)
                pe.wait_ge(s2_y2, EC * (b + 1))
                for t in range(LB):
                    for c in range(EC):
                        ins = pe.matmul(bank(t // 4)[:, P * (t % 4):P * (t % 4) + P], dl[:, c, P * t:P * t + P],
                                        owT[:, c, :], start=c == 0, stop=c == EC - 1)
                ins.then_inc(s2_o, 1)

        def s2_act(act, link, s):
            act.wait_ge(s2_wT, 1)
            act.activation(inT[0], bank(2)[:, 0:256], ACT.Copy).then_inc(s2_wc, 1)
            act.activation(skT[0], bank(2)[:, 256:512], ACT.Copy).then_inc(s2_wc, 1)
            act.activation(wd1T, bank(3)[:, 0:P].rearrange("p (c r) -> p c r", c=EC), ACT.Copy).then_inc(s2_wc, 1)
            act.activation(wd2T[0:DT], bank(3)[0:DT, P:P + E2], ACT.Copy).then_inc(s2_wc, 1)
            link(act.activation(negA, bank(3)[:, 384:384 + EC * NG], ACT.Exp))
            act.activation(negA, negA, ACT.Copy, scale=-1.0).then_inc(s2_wc, 1)
            act.activation(owT, bank(4)[:, 0:256].rearrange("p (c d) -> p c d", c=EC), ACT.Copy).then_inc(s2_wc, 1)
            for w, o in ((wbT, 256), (wcT, 320)):
                for c in range(EC):
                    act.activation(w[:, c, :].rearrange("p (e n) -> p e n", e=EG),
                                   bank(4)[:, o + NS * c:o + NS * c + NS].unsqueeze(1).to_broadcast([P, EG, NS]),
                                   ACT.Copy).then_inc(s2_wc, 1)
            ln_act(act, link, s)
            for b in range(B):
                wait(act, x_done, X_AFTER[s] + b)
                for n in range(8):
                    kind, c, i = n // 4, n // 2 % 2, n % 2
                    act.wait_ge(s2_in, 8 * b + n + 1)
                    if kind == 0:
                        act.activation(xp[:, c, KW - 1 + 512 * i:KW - 1 + 512 * i + 512], bank(6 + n % 2),
                                       ACT.Copy).then_inc(s2_ina, 1)
                    else:
                        act.activation(sk[:, c, 512 * i:512 * i + 512], bank(6 + n % 2), ACT.Silu).then_inc(s2_ina, 1)
                for c in range(EC):
                    act.wait_ge(s2_conv, 2 * b + c + 1)
                    act.activation(xc[:, c, :], uu[:, c, :], ACT.Silu, bias=cb[:, c:c + 1]).then_inc(s2_xc, 1)
                for i in range(2):
                    act.wait_ge(s2_dr, 2 * b + i + 1)
                    act.activation(dtr[0:DT, 0, 512 * i:512 * i + 512], bank(2 + i)[0:DT, :],
                                   ACT.Copy).then_inc(s2_drc, 1)
                for n in range(4):
                    act.wait_ge(s2_bc, 4 * b + n + 1)
                    act.activation((bb, cc)[n // 2][:, 512 * (n % 2):512 * (n % 2) + 512], bank(4 + n),
                                   ACT.Copy).then_inc(s2_bcc, 1)
                act.wait_ge(s2_xc, 2 * b + 2)
                for n in range(4):
                    c, i = n // 2, n % 2
                    act.wait_ge(s2_z, 4 * b + n + 1)
                    act.activation(sp_e[:, c, 512 * i:512 * i + 512], bank(n), ACT.Abs,
                                   bias=db[:, c:c + 1]).then_inc(s2_ab, 1)
                act.wait_ge(s2_ab, 4 * b + 4)
                for c in range(EC):
                    link(act.activation(sp_e[:, c, :], sp_e[:, c, :], ACT.Exp, scale=-1.0))
                for c in range(EC):
                    act.activation(sp_e[:, c, :], sp_e[:, c, :], ACT.Ln, bias=1.0).then_inc(s2_sp, 2)
                for c in range(EC):
                    act.wait_ge(s2_dl, 4 * b + 2 * c + 1)
                    act.activation(dlh[:, c, :], dl[:, c, :], ACT.Copy).then_inc(s2_hi, 1)
                for c in range(EC):
                    act.wait_ge(s2_dl, 4 * b + 2 * c + 2)
                    act.activation(dxh[:, c, :], dA[:, c, :], ACT.Copy).then_inc(s2_hi, 1)
                act.wait_ge(s2_lo, 4 * b + 4)
                for k in range(EC * NG):
                    kk = b * EC * NG + k
                    G = k // NG * NG + ORDER[k % NG]
                    for i in range(2):
                        v = 2 * kk + i
                        act.wait_ge(s2_pd, v + 1)
                        wait(act, s2_h, kk - 1)
                        act.activation(dA[:, kk % 2, 512 * i:512 * i + 512], bank(v % 3), ACT.Exp,
                                       scale=negA[:, G:G + 1]).then_inc(s2_dA, 1)

        def s2_dve(dve, link, s):
            dve.wait_ge(s2_wc, 10)
            dve.tensor_tensor(inT[1], bank(2)[:, 0:256], f32(inT[0]), ALU.subtract).then_inc(s2_wl, 1)
            dve.tensor_tensor(skT[1], bank(2)[:, 256:512], f32(skT[0]), ALU.subtract).then_inc(s2_wl, 1)
            ln_dve(dve, link, s)
            dve.wait_ge(s2_sel, 2)
            for b in range(B):
                for c in range(EC):
                    dve.wait_ge(s2_ina, 8 * b + 2 * c + 2)
                    link(dve.tensor_scalar(uu[:, c, :], xp[:, c, 0:L], cw[:, c, 0:1], None, ALU.mult))
                    for k in range(1, KW):
                        ins = dve.scalar_tensor_tensor(out=uu[:, c, :], in0=xp[:, c, k:k + L],
                                                       scalar=cw[:, c, k:k + 1], in1=uu[:, c, :],
                                                       op0=ALU.mult, op1=ALU.add)
                        if k < KW - 1:
                            link(ins)
                    ins.then_inc(s2_conv, 1)
                for n in range(4):
                    c, i = n // 2, n % 2
                    dve.wait_ge(s2_ab, 4 * b + n + 1)
                    ins = dve.tensor_scalar(dl[:, c, 512 * i:512 * i + 512], bank(n), db[:, c:c + 1], 0.0,
                                            ALU.add, ALU.max)
                    ins.then_inc(chain_dve, 1)
                    link.n += 1
                dve.wait_ge(chain_dve, link.n)
                dve.wait_ge(s2_sp, 4 * b + 4)
                for c in range(EC):
                    dve.tensor_tensor(dl[:, c, :], dl[:, c, :], sp_e[:, c, :], ALU.add).then_inc(s2_dl, 1)
                    dve.wait_ge(s2_dl, 4 * b + 2 * c + 1)
                    dve.tensor_tensor(dA[:, c, :], dl[:, c, :], xc[:, c, :], ALU.mult).then_inc(s2_dl, 1)
                    dve.wait_ge(s2_dl, 4 * b + 2 * c + 2)
                dve.wait_ge(s2_hi, 4 * b + 4)
                for c in range(EC):
                    dve.tensor_tensor(dll[:, c, :], dl[:, c, :], f32(dlh[:, c, :]), ALU.subtract).then_inc(s2_lo, 1)
                    dve.tensor_tensor(dxl[:, c, :], dA[:, c, :], f32(dxh[:, c, :]), ALU.subtract).then_inc(s2_lo, 1)
                dve.wait_ge(s2_lo, 4 * b + 4)
                dve.wait_ge(s2_bcc, 4 * b + 4)

                def gate(c):
                    dve.wait_ge(s2_yg, b * EC * NG + (c + 1) * NG)
                    link(dve.scalar_tensor_tensor(out=dl[:, c, :], in0=xc[:, c, :], scalar=wdd[:, c:c + 1],
                                                  in1=bank(6, 2), op0=ALU.mult, op1=ALU.add))
                    dve.tensor_tensor(dl[:, c, :], dl[:, c, :], sk[:, c, :], ALU.mult).then_inc(s2_y2, 1)

                for k in range(EC * NG):
                    kk = b * EC * NG + k
                    wait(dve, s2_h, kk - 1)
                    for i in range(2):
                        v = 2 * kk + i
                        dve.wait_ge(s2_pd, v + 1)
                        dve.tensor_tensor(uu[:, kk % 2, 512 * i:512 * i + 512], bank(3 + v % 3),
                                          bb[:, 512 * i:512 * i + 512], ALU.mult).then_inc(s2_u, 1)
                    dve.wait_ge(s2_u, 2 * kk + 2)
                    dve.wait_ge(s2_dA, 2 * kk + 2)
                    wait(dve, s2_hc, kk - 1)
                    dve.tensor_tensor_scan(hs[:, kk % 2, :], dA[:, kk % 2, :], uu[:, kk % 2, :], 0.0,
                                           ALU.mult, ALU.add).then_inc(s2_h, 1)
                    if k % NG == 1 and k > NG:
                        gate(k // NG - 1)
                gate(EC - 1)
                dve.wait_ge(s2_o, b + 1)
                xb = X[:, LB * b:LB * b + LB, :].rearrange("p t d -> p (t d)")
                rb_ = R[:, LB * b:LB * b + LB, :].rearrange("p t d -> p (t d)")
                link(dve.tensor_tensor(xb, xb, bank(0, 2), ALU.add))
                dve.tensor_tensor(xb, xb, rb_, ALU.add).then_inc(x_done, 1)
                dve.wait_ge(x_done, X_AFTER[s] + b + 1)

        H4, HD4 = 4, 32
        tf, tr = carver(AF, AF_WORDS), carver(AR, AR_WORDS)
        w4_raw = tf(3 * D)
        wo4_raw = tf(D)
        wq4T = tf(P)
        bout4 = tf(D)
        head_mask = tf(P)
        k4e = tf(L)
        k4t = tf(LB, P)
        v4 = tf(LB, P)
        ctxm = tf(P)
        m2 = tf(P)
        k4m = tf(2)
        k4s = tf(2)
        k4r = tf(2)
        w4h, w4l = tr(3 * D), tr(3 * D)
        g4h, g4l = tr(P), tr(P)

        s4_w = sem("s4_w")
        s4_wt = sem("s4_wt")
        s4_wh = sem("s4_wh")
        s4_wl = sem("s4_wl")
        s4_mask = sem("s4_mask")
        s4_k = sem("s4_k")
        s4_m = sem("s4_m")
        s4_e = sem("s4_e")
        s4_v = sem("s4_v")
        s4_vc = sem("s4_vc")
        s4_kt = sem("s4_kt")
        s4_ktc = sem("s4_ktc")
        s4_c = sem("s4_c")
        s4_cm = sem("s4_cm")
        s4_y = sem("s4_y")

        def s4_load(q, s):
            q.wait_ge(x_done, X_AFTER[s])
            q.dma_start(w4_raw, a["L1_attn_a_w_qkv"]).then_inc(s4_w, 16)
            q.dma_start(wo4_raw, a["L1_attn_a_w_out"]).then_inc(s4_w, 16)
            q.dma_start(bout4[0:1], a["L1_attn_a_b_out"].rearrange("(a d) -> a d", a=1)).then_inc(s4_w, 16)

        def s4_pool(pool, link, s):
            pool.wait_ge(x_done, X_AFTER[s])
            link(pool.memset(head_mask, 0.0))
            for h in range(H4):
                r = HD4 * h
                pool.memset(head_mask[r:r + HD4, r:r + HD4], 1.0).then_inc(s4_mask, 1)

        def s4_pe(pe, s):
            pe.wait_ge(s4_w, 48)
            pe.transpose(bank(2)[:, 0:P], w4_raw[:, 0:D], ident[:, :]).then_inc(s4_wt, 1)
            ln_pe(pe, s)
            pe.wait_ge(s4_wl, 1)
            for b in range(B):
                wait(pe, x_done, X_AFTER[s] + b)
                for i in range(2):
                    pe.wait_ge(ln_lo, 4 * s + 2 * b + i + 1)
                    ins = mm3(pe, bank(4 + i), (w4h[:, D:2 * D], w4l[:, D:2 * D]), xt(L * b + 512 * i, 512))
                ins.then_inc(s4_k, 1)
                for t in range(LB):
                    ins = mm3(pe, bank(6 + t // 4)[:, P * (t % 4):P * (t % 4) + P], xt(L * b + P * t, P),
                              (w4h[:, 2 * D:3 * D], w4l[:, 2 * D:3 * D]))
                ins.then_inc(s4_v, 1)
                pe.wait_ge(s4_e, b + 1)
                for t in range(LB):
                    ins = pe.transpose(bank(4 + t // 4)[:, P * (t % 4):P * (t % 4) + P], k4e[:, P * t:P * t + P],
                                       ident[:, :])
                ins.then_inc(s4_kt, 1)
                pe.wait_ge(s4_vc, b + 1)
                pe.wait_ge(s4_ktc, b + 1)
                for t in range(LB):
                    ins = pe.matmul(bank(2)[:, 0:P], v4[:, t, :], k4t[:, t, :], start=t == 0, stop=t == LB - 1)
                ins.then_inc(s4_c, 1)
                pe.wait_ge(s4_cm, 4 * b + 1)
                pe.matmul(bank(3)[:, 0:P], ctxm, wo4_raw, start=True, stop=True).then_inc(s4_c, 1)
                pe.wait_ge(s4_cm, 4 * b + 2)
                pe.matmul(bank(2)[:, 0:P], wq4T, m2, start=True, stop=True).then_inc(s4_c, 1)
                pe.wait_ge(s4_cm, 4 * b + 4)
                for t in range(LB):
                    o = bank(6 + t // 4)[:, P * (t % 4):P * (t % 4) + P]
                    mm3(pe, o, xt(L * b + P * t, P), (g4h, g4l), stop=False)
                    ins = pe.matmul(o, ones_row[0:1, :], bout4[0:1, :], start=False, stop=True)
                ins.then_inc(s4_y, 1)

        def s4_act(act, link, s):
            act.wait_ge(s4_w, 48)
            act.activation(w4h, w4_raw, ACT.Copy).then_inc(s4_wh, 1)
            act.wait_ge(s4_wt, 1)
            act.activation(wq4T, bank(2)[:, 0:P], ACT.Copy).then_inc(s4_wh, 1)
            ln_act(act, link, s)
            for b in range(B):
                act.wait_ge(s4_m, b + 1)
                act.activation(k4e, bank(4, 2), ACT.Exp, bias=k4m[:, b:b + 1],
                               accum_out=k4s[:, b:b + 1]).then_inc(s4_e, 1)
                act.wait_ge(s4_v, b + 1)
                act.activation(v4.rearrange("p t d -> p (t d)"), bank(6, 2), ACT.Copy).then_inc(s4_vc, 1)
                act.wait_ge(s4_c, 3 * b + 3)
                act.activation(g4h, bank(2)[:, 0:P], ACT.Copy).then_inc(s4_cm, 1)

        def s4_dve(dve, link, s):
            dve.wait_ge(s4_wh, 2)
            dve.tensor_tensor(w4l, w4_raw, f32(w4h), ALU.subtract).then_inc(s4_wl, 1)
            ln_dve(dve, link, s)
            for b in range(B):
                dve.wait_ge(s4_k, b + 1)
                dve.tensor_reduce(k4m[:, b:b + 1], bank(4, 2), AX, ALU.max, negate=True).then_inc(s4_m, 1)
                dve.wait_ge(s4_e, b + 1)
                link(dve.reciprocal(k4r[:, b:b + 1], k4s[:, b:b + 1]))
                dve.wait_ge(s4_kt, b + 1)
                dve.tensor_copy(k4t.rearrange("p t d -> p (t d)"), bank(4, 2)).then_inc(s4_ktc, 1)
                dve.wait_ge(s4_c, 3 * b + 1)
                dve.wait_ge(s4_mask, H4)
                dve.tensor_tensor(ctxm, bank(2)[:, 0:P], head_mask, ALU.mult).then_inc(s4_cm, 1)
                dve.wait_ge(s4_c, 3 * b + 2)
                dve.tensor_scalar(m2, bank(3)[:, 0:P], k4r[:, b:b + 1], HD4 ** -0.5, ALU.mult,
                                  ALU.mult).then_inc(s4_cm, 1)
                dve.wait_ge(s4_cm, 4 * b + 3)
                dve.tensor_tensor(g4l, bank(2)[:, 0:P], f32(g4h), ALU.subtract).then_inc(s4_cm, 1)
                dve.wait_ge(s4_y, b + 1)
                xb = X[:, LB * b:LB * b + LB, :].rearrange("p t d -> p (t d)")
                rb_ = R[:, LB * b:LB * b + LB, :].rearrange("p t d -> p (t d)")
                link(dve.tensor_tensor(xb, xb, bank(6, 2), ALU.add))
                dve.tensor_tensor(xb, xb, rb_, ALU.add).then_inc(x_done, 1)
                dve.wait_ge(x_done, X_AFTER[s] + b + 1)

        H6, HD6 = 16, 8
        HS = 4
        SS = H6 // HS
        SUB = 64
        SC6 = HD6 ** -0.5
        POOL_HEADS = 15
        LAG = 4
        TILES = [(g, kb) for g in range(NB) for kb in range(LB)]
        NTI = len(TILES)
        tf, tr = carver(AF, AF_WORDS), carver(AR, AR_WORDS)
        w6_raw = tf(3 * D)
        b6_raw = tf(3 * D)
        wp6 = tf(SS, D)
        bp6 = tf(D)
        b6rep = tf(2 * SS, P)
        ones6 = tf(512)
        lo_q = tf(1)
        lo_k = tf(1)
        tmp6 = tf(2, 512)
        v6 = tf(NB, P)
        e6_a = tf(3, H6 * P)
        p6_a = tf(2, H6 * P)
        z6 = tf(2, P)
        lnz = tf(P)
        w6i = tf(2, P)
        ot6 = tf(2, 512)
        rep_h = tr(2 * SS, P)
        rep_l = tr(2 * SS, P)
        wv_h, wv_l = tr(P), tr(P)
        hi6 = tr(2, 512)
        k6 = tr(SS, T)
        q6 = tr(3, SS * HS * P)
        negm6 = ctx.enter_context(nc.sbuf_tensor("negm6", [P, 4, SUB], BF16))
        e6 = [e6_a[:, 0, :], e6_a[:, 1, :], e6_a[:, 2, :], XN[:, :, :].rearrange("p t d -> p (t d)")]
        p6 = [p6_a[:, 0, :], p6_a[:, 1, :], hc[:, :, :].rearrange("p a b -> p (a b)")]

        s6_w = sem("s6_w")
        s6_z = sem("s6_z")
        s6_wp = sem("s6_wp")
        s6_wh = sem("s6_wh")
        s6_wl = sem("s6_wl")
        s6_pr = sem("s6_pr")
        s6_tmp = sem("s6_tmp")
        s6_hi = sem("s6_hi")
        s6_st = sem("s6_st")
        s6_sc = sem("s6_sc")
        s6_s = sem("s6_s")
        s6_max = sem("s6_max")
        s6_sub = sem("s6_sub")
        s6_e = sem("s6_e")
        s6_zs = sem("s6_zs")
        s6_wi = sem("s6_wi")
        s6_pd = sem("s6_pd")
        s6_pp = sem("s6_pp")
        s6_pv = sem("s6_pv")
        s6_ot = sem("s6_ot")
        s6_o = sem("s6_o")

        def kv_jobs(b):
            return [("k", b, x, i) for x in range(SS) for i in range(2)] + [("v", b, i) for i in range(2)]

        JOBS = [(job, None) for job in kv_jobs(0) + [("q", 0), ("q", 1)]]
        for g in range(NB - 2):
            JOBS.append((("q", g + 2), LB * g + 2))
            rest = kv_jobs(1)
            if 1 <= g <= 5:
                JOBS.append((rest[2 * g - 2], LB * g + 4))
                JOBS.append((rest[2 * g - 1], LB * g + 6))
        JOBS = [(n, job, at) for n, (job, at) in enumerate(JOBS)]

        def queries_before(n):
            return sum(1 for _, job, _ in JOBS[:max(n, 0)] if job[0] == "q")

        FIRST_JOBS = [j for j in JOBS if j[2] is None]
        JOBS_AT = {at: (n, job) for n, job, at in JOBS if at is not None}

        def jobs_before(t):
            return sum(1 for _, _, at in JOBS if at is None or at < t)

        def job_bank(n, at):
            return bank(n % 2) if at is None else bank(6 + (at // LB + 1) % 2)

        def s6_load(q, s):
            q.wait_ge(x_done, X_AFTER[s])
            q.dma_start(w6_raw, a["L1_attn_b_w_qkv"]).then_inc(s6_w, 16)
            q.dma_start(b6_raw[0:1], a["L1_attn_b_b_qkv"].rearrange("(a d) -> a d", a=1)).then_inc(s6_w, 16)
            q.dma_start(bp6[0:1], a["L1_attn_b_b_proj"].rearrange("(a d) -> a d", a=1)).then_inc(s6_w, 16)
            q.wait_ge(s6_z, 4)
            for i in range(HS):
                q.dma_start(wp6[32 * i:32 * i + HD6, :, :],
                            a["L1_attn_b_w_proj"].rearrange("(x i d) c -> i d x c", x=SS, i=HS)[i]).then_inc(s6_wp, 16)

        def s6_pool(pool, link, s):
            pool.wait_ge(x_done, X_AFTER[s])
            pool.memset(wp6, 0.0).then_inc(s6_z, 1)
            pool.memset(q6.rearrange("p a b -> p (a b)").bitcast(F32), 0.0).then_inc(s6_z, 1)
            pool.memset(ot6, 0.0).then_inc(s6_z, 1)
            pool.memset(ones6[0:1], 1.0).then_inc(s6_z, 1)
            for m in range(NTI):
                pool.wait_ge(s6_wi, m + 1)
                wait(pool, s6_pv, m - 2)
                n = POOL_HEADS
                pool.tensor_tensor(p6[m % 3][:, 0:n * P].rearrange("p (h q) -> p h q", h=n),
                                   e6[m % 4][:, 0:n * P].rearrange("p (h q) -> p h q", h=n),
                                   w6i[:, m % 2, :].unsqueeze(1).to_broadcast([P, n, P]),
                                   ALU.mult).then_inc(s6_pp, 1)

        def s6_pe(pe, s):
            ln_pe(pe, s)
            pe.wait_ge(s6_wl, 2)
            pe.wait_ge(s6_z, 4)
            pe.wait_ge(ln_lo, 4 * s + 4)

            def make(n, job, at):
                wait(pe, s6_tmp, n - 1 if at is None else n)
                if at is not None and job[0] == "q":
                    wait(pe, x_done, X_AFTER[s] + at // LB)
                o = job_bank(n, at)
                if job[0] == "k":
                    _, b, x, i = job
                    mm3(pe, o, (rep_h[:, SS + x, :], rep_l[:, SS + x, :]), xt(L * b + 512 * i, 512), stop=False)
                    ins = pe.matmul(o, b6rep[0:1, SS + x, :], ones6[0:1, :], start=False, stop=True)
                elif job[0] == "v":
                    _, b, i = job
                    for t in range(4):
                        oo = o[:, P * t:P * t + P]
                        mm3(pe, oo, xt(L * b + 512 * i + P * t, P), (wv_h, wv_l), stop=False)
                        ins = pe.matmul(oo, ones6[0:1, 0:P], b6_raw[0:1, 2 * D:3 * D], start=False, stop=True)
                else:
                    for x in range(SS):
                        oo = o[:, P * x:P * x + P]
                        mm3(pe, oo, (rep_h[:, x, :], rep_l[:, x, :]), xt(P * job[1], P), stop=False)
                        ins = pe.matmul(oo, b6rep[0:1, x, :], ones6[0:1, 0:P], start=False, stop=True)
                ins.then_inc(s6_pr, 1)

            for n, job, at in FIRST_JOBS:
                make(n, job, at)

            def scores(j):
                g, kb = TILES[j // 2]
                if j % (2 * LB) == 0:
                    pe.wait_ge(s6_sc, g + 1)
                    pe.wait_ge(s6_st, jobs_before(LB * g - LAG - 2))
                wait(pe, s6_e, j - 2)
                k0 = L * (g // LB) + P * kb
                for x in range(SS):
                    q = q6[:, g % 3, :].rearrange("p (x i q) -> p x i q", x=SS, i=HS)[:, x]
                    q0 = SUB * (j % 2)
                    ins = pe.matmul(bank(2 * (j % 3) + x // 2)[:, 256 * (x % 2):256 * (x % 2) + 256],
                                    k6[:, x, k0:k0 + P], q[:, :, q0:q0 + SUB],
                                    start=x % 2 == 0, stop=True, skip_group_check=True)
                ins.then_inc(s6_s, 1)

            def subtract(j):
                pe.wait_ge(s6_max, j + 1)
                for h in range(2):
                    ins = pe.matmul(bank(2 * (j % 3) + h).rearrange("p (h q) -> p h q", h=8), ident_bf[:, :],
                                    negm6[:, j % 4, :].unsqueeze(1).to_broadcast([P, 8, SUB]), start=False,
                                    stop=True, skip_group_check=True)
                ins.then_inc(s6_sub, 1)

            def project(g):
                pe.wait_ge(s6_ot, g + 1)
                o = bank(6 + g % 2)[:, 0:P]
                for x in range(SS):
                    pe.matmul(o, ot6[:, g % 2, P * x:P * x + P], wp6[:, x, :], start=x == 0, stop=False)
                pe.matmul(o, ones_row[0:1, :], bp6[0:1, :], start=False, stop=True).then_inc(s6_o, 1)

            def pv(m, part):
                g, kb = TILES[m]
                if part == 0:
                    pe.wait_ge(s6_pp, m + 1)
                    pe.wait_ge(s6_pd, m + 1)
                    if kb == 0:
                        wait(pe, s6_tmp, jobs_before(m))
                        wait(pe, x_done, X_AFTER[s] + g - 1)
                for x in (2 * part, 2 * part + 1):
                    for i in range(HS):
                        h = HS * x + i
                        ins = pe.matmul(bank(6 + g % 2)[32 * i:32 * i + HD6, P * x:P * x + P],
                                        v6[:, LB * (g // LB) + kb, HD6 * h:HD6 * h + HD6],
                                        p6[m % 3][:, P * h:P * h + P],
                                        start=kb == 0 and x == 0, stop=kb == LB - 1, skip_group_check=True)
                if part == 1:
                    ins.then_inc(s6_pv, 1)
                    if kb == 0 and m:
                        project(g - 1)
                    if m in JOBS_AT:
                        make(*JOBS_AT[m], m)
                    if m == NTI - 1:
                        project(g)

            pe.wait_ge(s6_wp, 16 * HS)
            scores(0)
            scores(1)
            for j in range(2 * NTI):
                subtract(j)
                if j + 2 < 2 * NTI:
                    scores(j + 2)
                if j // 2 >= LAG:
                    pv(j // 2 - LAG, j % 2)
            for m in range(NTI - LAG, NTI):
                pv(m, 0)
                pv(m, 1)

        def s6_act(act, link, s):
            act.preload_act_table_set("natural_log_exp_and_others")
            act.wait_ge(s6_w, 48)
            for kind in range(2):
                src = w6_raw[:, D * kind:D * kind + D].rearrange("p (x i d) -> p x i d", x=SS, i=HS)
                bsrc = b6_raw[0:1, D * kind:D * kind + D].rearrange("p (x i d) -> p x i d", x=SS, i=HS)
                for x in range(SS):
                    w = SS * kind + x
                    act.activation(rep_h[:, w, :].rearrange("p (i c d) -> p i c d", i=HS, c=4),
                                   src[:, x].unsqueeze(2).to_broadcast([P, HS, 4, HD6]),
                                   ACT.Copy).then_inc(chain_act, 1)
                    act.activation(b6rep[0:1, w, :].rearrange("p (i c d) -> p i c d", i=HS, c=4),
                                   bsrc[:, x].unsqueeze(2).to_broadcast([1, HS, 4, HD6]),
                                   ACT.Copy).then_inc(chain_act, 1)
                    link.n += 2
            link(act.activation(wv_h, w6_raw[:, 2 * D:3 * D], ACT.Copy))
            act.sem_inc(s6_wh, 1)
            ln_act(act, link, s)

            def take(n, job, at):
                act.wait_ge(s6_pr, n + 1)
                o = job_bank(n, at)
                if job[0] == "v":
                    act.activation(v6[:, LB * job[1] + 4 * job[2]:LB * job[1] + 4 * job[2] + 4, :].rearrange(
                        "p t d -> p (t d)"), o, ACT.Copy).then_inc(s6_tmp, 1)
                    act.wait_ge(s6_tmp, n + 1)
                    act.wait_ge(s6_hi, n)
                    act.sem_inc(s6_hi, 1)
                    return
                wait(act, s6_st, n - 1)
                act.activation(tmp6[:, n % 2, :], o, ACT.Copy,
                               scale=SC6 if job[0] == "q" else 1.0).then_inc(s6_tmp, 1)
                act.wait_ge(s6_tmp, n + 1)
                wait(act, s6_sc, queries_before(n - 1))
                act.activation(hi6[:, n % 2, :], tmp6[:, n % 2, :], ACT.Copy).then_inc(s6_hi, 1)

            def scatter(n, job, at):
                if job[0] != "q":
                    return
                act.wait_ge(s6_st, n + 1)
                g = job[1]
                wait(act, s6_s, 2 * LB * (g - 2))
                for i in range(HS):
                    r = slice(32 * i, 32 * i + 32)
                    o = q6[r, g % 3, :].rearrange("p (x i q) -> p x i q", x=SS, i=HS)[:, :, i, :]
                    act.activation(o, f32(hi6[r, n % 2, :]).rearrange("p (x q) -> p x q", x=SS),
                                   ACT.Copy).then_inc(chain_act if i < HS - 1 else s6_sc, 1)
                link.n += HS - 1

            for n, job, at in FIRST_JOBS:
                take(n, job, at)
            for n, job, at in FIRST_JOBS:
                scatter(n, job, at)

            def invert(m):
                act.wait_ge(s6_zs, m + 1)
                wait(act, s6_wi, m)
                link(act.activation(lnz, z6[:, m % 2, :], ACT.Ln))
                wait(act, s6_pp, m - 1)
                wait(act, s6_pd, m - 1)
                act.activation(w6i[:, m % 2, :], lnz, ACT.Exp, scale=-1.0).then_inc(s6_wi, 1)

            def flush(g):
                act.wait_ge(s6_pv, LB * (g + 1))
                act.wait_ge(s6_z, 4)
                wait(act, s6_o, g - 1)
                for i in range(HS):
                    r = 32 * i
                    act.activation(ot6[r:r + HD6, g % 2, :], bank(6 + g % 2)[r:r + HD6],
                                   ACT.Copy).then_inc(chain_act if i < HS - 1 else s6_ot, 1)
                link.n += HS - 1

            for j in range(2 * NTI):
                act.wait_ge(s6_sub, j + 1)
                if j % 2 == 0:
                    wait(act, s6_pp, j // 2 - 3)
                    wait(act, s6_pd, j // 2 - 3)
                o = e6[j // 2 % 4].rearrange("p (h q) -> p h q", h=H6)
                q0 = SUB * (j % 2)
                act.activation(o[:, :, q0:q0 + SUB], bank(2 * (j % 3), 2).rearrange("p (h q) -> p h q", h=H6),
                               ACT.Exp).then_inc(s6_e, 1)
                if j % 2 == 0 and j >= 4:
                    invert(j // 2 - 2)
                m = j // 2 - LAG
                if j % 2 and m >= 0:
                    if m % LB == LB - 1:
                        flush(m // LB)
                    if m - 1 in JOBS_AT:
                        take(*JOBS_AT[m - 1], m - 1)
                    if m - 3 in JOBS_AT:
                        scatter(*JOBS_AT[m - 3], m - 3)
            invert(NTI - 2)
            invert(NTI - 1)
            flush(NB - 1)

        def s6_dve(dve, link, s):
            dve.wait_ge(s6_wh, 1)
            for kind in range(2):
                src = w6_raw[:, D * kind:D * kind + D].rearrange("p (x i d) -> p x i d", x=SS, i=HS)
                for x in range(SS):
                    w = SS * kind + x
                    ins = dve.tensor_tensor(rep_l[:, w, :].rearrange("p (i c d) -> p i c d", i=HS, c=4),
                                            src[:, x].unsqueeze(2).to_broadcast([P, HS, 4, HD6]),
                                            f32(rep_h[:, w, :]).rearrange("p (i c d) -> p i c d", i=HS, c=4),
                                            ALU.subtract)
                    if w < 2 * SS - 1:
                        ins.then_inc(chain_dve, 1)
                        link.n += 1
            ins.then_inc(s6_wl, 1)
            dve.tensor_tensor(wv_l, w6_raw[:, 2 * D:3 * D], f32(wv_h), ALU.subtract).then_inc(s6_wl, 1)
            idq = ident[:, :].rearrange("p (i r) -> p i r", i=HS)[:, :, 16:32]
            idk = ident[:, :].rearrange("p (i r) -> p i r", i=2 * HS)[:, :, 8:16]
            link(dve.tensor_reduce(lo_q, idq, mybir.AxisListType.XY, ALU.add, negate=True))
            link(dve.tensor_reduce(lo_k, idk, mybir.AxisListType.XY, ALU.add, negate=True))
            ln_dve(dve, link, s)
            dve.wait_ge(s6_z, 4)

            def stack(n, job, at):
                dve.wait_ge(s6_hi, n + 1)
                if job[0] == "v":
                    wait(dve, s6_st, n)
                    dve.sem_inc(s6_st, 1)
                elif job[0] == "k":
                    _, b, x, i = job
                    dve.scalar_tensor_tensor(out=k6[:, x, L * b + 512 * i:L * b + 512 * i + 512],
                                             in0=f32(hi6[:, n % 2, :]), scalar=lo_k, in1=tmp6[:, n % 2, :],
                                             op0=ALU.mult, op1=ALU.add).then_inc(s6_st, 1)
                else:
                    h = hi6[:, n % 2, :]
                    dve.scalar_tensor_tensor(out=h, in0=f32(h), scalar=lo_q, in1=tmp6[:, n % 2, :],
                                             op0=ALU.mult, op1=ALU.add).then_inc(s6_st, 1)

            for n, job, at in FIRST_JOBS:
                stack(n, job, at)

            def maxima(j):
                dve.wait_ge(s6_s, j + 1)
                wait(dve, s6_sub, j - 3)
                dve.tensor_reduce(negm6[:, j % 4, :], bank(2 * (j % 3), 2).rearrange("p (h q) -> p q h", h=H6), AX,
                                  ALU.max, negate=True).then_inc(s6_max, 1)

            def denominators(m):
                dve.wait_ge(s6_e, 2 * m + 2)
                wait(dve, s6_wi, m - 1)
                dve.tensor_reduce(z6[:, m % 2, :], e6[m % 4].rearrange("p (h q) -> p q h", h=H6), AX,
                                  ALU.add).then_inc(s6_zs, 1)

            def normalise(m):
                dve.wait_ge(s6_wi, m + 1)
                wait(dve, s6_pv, m - 2)
                n = H6 - POOL_HEADS
                e = e6[m % 4].rearrange("p (h q) -> p h q", h=H6)
                dve.tensor_tensor(p6[m % 3][:, POOL_HEADS * P:].rearrange("p (h q) -> p h q", h=n),
                                  e[:, POOL_HEADS:, :], w6i[:, m % 2, :].unsqueeze(1).to_broadcast([P, n, P]),
                                  ALU.mult).then_inc(s6_pd, 1)

            def add(g):
                dve.wait_ge(s6_o, g + 1)
                dve.tensor_tensor(X[:, g, :], X[:, g, :], bank(6 + g % 2)[:, 0:P], ALU.add).then_inc(x_done, 1)

            for j in range(2 * NTI):
                maxima(j)
                if j % 2 and j >= 3:
                    denominators(j // 2 - 1)
                    if j >= 5:
                        normalise(j // 2 - 2)
                    m = j // 2 - LAG - 1
                    if m > 0 and m % LB == 0:
                        add(m // LB - 1)
                    if m - 1 in JOBS_AT:
                        stack(*JOBS_AT[m - 1], m - 1)
            denominators(NTI - 1)
            normalise(NTI - 2)
            normalise(NTI - 1)
            add(NB - 1)
            dve.wait_ge(x_done, X_AFTER[s + 1])

        PE = {0: s0_pe, 1: s1_pe, 2: s2_pe, 3: s1_pe, 4: s4_pe, 5: moe_pe, 6: s6_pe, 7: moe_pe}
        ACTS = {0: s0_act, 1: s1_act, 2: s2_act, 3: s1_act, 4: s4_act, 5: moe_act, 6: s6_act, 7: moe_act}
        DVE = {0: s0_dve, 1: s1_dve, 2: s2_dve, 3: s1_dve, 4: s4_dve, 5: moe_dve, 6: s6_dve, 7: moe_dve}
        POOL = {2: s2_pool, 4: s4_pool, 6: s6_pool}
        LOAD = {1: s1_load, 2: s2_load, 3: s1_load, 4: s4_load, 5: moe_load, 6: s6_load, 7: moe_load}
        X_AFTER = {1: 2, 2: 6, 3: 8, 4: 12, 5: 14, 6: 18, 7: 34, 8: 38}

        block = ctx.enter_context(nc.Block())

        @block.sync
        def _(sp):
            sp.dma_start(X[:, :, :], x_dram).then_inc(x_loaded, 16)
            s0_load(sp)
            for s in range(1, upto):
                LOAD[s](sp, s)
            sp.wait_ge(x_done, X_AFTER[upto])
            sp.dma_start(out_dram, X[:, :, :]).then_inc(out_sem, 16)
            sp.wait_ge(out_sem, 16)

        @block.gpsimd
        def _(pool):
            link = Chain(pool, chain_pool)
            link(pool.memset(ident[:, :], 0.0))
            link(pool.affine_select(out=ident[:, :], in_=ident[:, :], compare_op=ALU.not_equal, fill=1.0,
                                    base=0, pattern=[[-1, P]], channel_multiplier=1))
            link(pool.tensor_copy(ident_bf[:, :], ident[:, :]))
            link(pool.memset(causal_bf[:, :], 0.0))
            link(pool.affine_select(out=causal_bf[:, :], in_=causal_bf[:, :], compare_op=ALU.is_ge, fill=MASKED,
                                    base=0, pattern=[[-1, P]], channel_multiplier=1))
            link(pool.memset(half_pow[:, :], -0.5))
            pool.memset(ones_row[:, :], 1.0).then_inc(consts_ready, 1)
            for s in range(upto):
                ln_pool(pool, link, s)
                if s in POOL:
                    POOL[s](pool, link, s)

        @block.tensor
        def _(pe):
            for s in range(upto):
                PE[s](pe) if s == 0 else PE[s](pe, s)

        @block.scalar
        def _(act):
            link = Chain(act, chain_act)
            for s in range(upto):
                ACTS[s](act, link) if s == 0 else ACTS[s](act, link, s)

        @block.vector
        def _(dve):
            link = Chain(dve, chain_dve)
            for s in range(upto):
                DVE[s](dve, link) if s == 0 else DVE[s](dve, link, s)


_INS = ['L0_attn_a_x_bld', 'L0_attn_a_Wq', 'L0_attn_a_Wkv_down', 'L0_attn_a_Wk_up', 'L0_attn_a_Wv_up',
        'L0_attn_a_Wout', 'L0_attn_b_norm_w', 'L0_attn_b_skip_w', 'L0_attn_b_in_w', 'L0_attn_b_conv_w',
        'L0_attn_b_conv_b', 'L0_attn_b_wd1', 'L0_attn_b_wd2', 'L0_attn_b_wd2_b', 'L0_attn_b_wb', 'L0_attn_b_wc',
        'L0_attn_b_A_log', 'L0_attn_b_W_D', 'L0_attn_b_out_w', 'L0_ffn_W_fc', 'L0_ffn_W_proj',
        'L1_attn_a_gamma', 'L1_attn_a_beta', 'L1_attn_a_w_qkv', 'L1_attn_a_w_out', 'L1_attn_a_b_out',
        'L1_attn_b_w_qkv', 'L1_attn_b_b_qkv', 'L1_attn_b_w_proj', 'L1_attn_b_b_proj',
        'L1_ffn_Wg', 'L1_ffn_Wu', 'L1_ffn_Wd']


def kernel(**inputs):
    import numpy as np
    import concourse.bacc as bacc
    from concourse.bass_utils import run_bass_kernel_spmd as run

    nc = bacc.Bacc("TRN2", target_bir_lowering=False, num_devices=1)
    arrays, a = {}, {}
    for name in _INS:
        v = np.ascontiguousarray(inputs[name])
        arrays[f"in_{name}_dram"] = v
        a[name] = nc.dram_tensor(f"in_{name}_dram", v.shape, mybir.dt.from_np(v.dtype), kind="ExternalInput").ap()
    out = nc.dram_tensor("out_dram", (B, L, D), F32, kind="ExternalOutput").ap()
    build(nc, a, out)
    r = run(nc, [arrays], core_ids=[0])
    return r.results[0]["out_dram"]
```
